# Optimizing a Trainium2 kernel written in Bass

```python
import numpy as np
import jax
import jax.numpy as jnp

def _softmax(x, axis=-1):
    return jax.nn.softmax(x, axis=axis)

def _gelu(x):
    return jax.nn.gelu(x, approximate=True)

def _silu(x):
    return jax.nn.silu(x)

def _sigmoid(x):
    return jax.nn.sigmoid(x)

def _layernorm(x, axis=-1, eps=1e-05):
    m = jnp.mean(x, axis=axis, keepdims=True)
    v = jnp.var(x, axis=axis, keepdims=True)
    return (x - m) / jnp.sqrt(v + eps)

def _scatter_add(tgt, idx, src, axis=0):
    return tgt.at[idx].add(src)

def _segment_sum(src, seg, n):
    return jax.ops.segment_sum(src, seg, n)
kernel_name = 'mk_seq_preln_d2_jaxref_r8_6b8b0d'

def setup_inputs(seed: int=0):
    np.random.seed(seed)
    _w = jnp.asarray

    def _L0_attn_setup():
        import jax, jax.numpy as jnp
        import numpy as np
        NUM_HEAD = 16
        D_Q = 64
        D_KV = 64
        ROPE_BASE = 10000.0

        def _cos_sin(seq_len, dim):
            pos = jnp.arange(seq_len, dtype=jnp.float32)[:, None]
            ids = jnp.arange(dim // 2, dtype=jnp.float32)
            theta = ROPE_BASE ** (-2.0 * ids) / (dim // 2)
            r = pos * theta[None, :]
            return (jnp.cos(r), jnp.sin(r))

        def _rope(x, cos, sin):
            b, s, d = x.shape
            xv = x.reshape(b, s, d // 2, 2)
            x0, x1 = (xv[..., 0], xv[..., 1])
            out = jnp.stack([x0 * cos - x1 * sin, x1 * cos + x0 * sin], axis=-1)
            return out.reshape(b, s, d)
        key = jax.random.key(seed)
        ks = jax.random.split(key, 10)
        d_model, d_q, d_kv = (128, D_Q, D_KV)
        b, s = (2, 256)
        w = lambda k, i, o: jax.random.normal(k, (i, o), dtype=jnp.float32) * 0.02
        return {'x': jax.random.normal(ks[0], (b, s, d_model), dtype=jnp.float32), 'Wd_q_w': w(ks[1], d_model, d_q), 'Wd_q_b': jnp.zeros((d_q,), jnp.float32), 'Wu_q_w': w(ks[2], d_q, d_model), 'Wu_q_b': jnp.zeros((d_model,), jnp.float32), 'Wq_r_w': w(ks[3], d_q, d_model), 'Wq_r_b': jnp.zeros((d_model,), jnp.float32), 'Wk_r_w': w(ks[4], d_model, d_model), 'Wk_r_b': jnp.zeros((d_model,), jnp.float32), 'Wd_kv_w': w(ks[5], d_model, d_kv), 'Wd_kv_b': jnp.zeros((d_kv,), jnp.float32), 'Wu_k_w': w(ks[6], d_kv, d_model), 'Wu_k_b': jnp.zeros((d_model,), jnp.float32), 'Wu_v_w': w(ks[7], d_kv, d_model), 'Wu_v_b': jnp.zeros((d_model,), jnp.float32), 'Wo_w': w(ks[8], d_model, d_model), 'Wo_b': jnp.zeros((d_model,), jnp.float32)}
    _L0_attn_in = _L0_attn_setup()

    def _L0_ffn_setup():
        import jax, jax.numpy as jnp
        import numpy as np
        DIM = 128
        DEPTH = 6
        HEADS = 16
        DIM_HEAD = 64
        WINDOW = 32
        INNER = HEADS * DIM_HEAD
        DIM_INNER = int(DIM * 4 * 2 / 3)
        QK_SCALE = 8.0

        def shift_tokens(t):
            a, s = jnp.split(t, 2, -1)
            s = jnp.pad(s, ((0, 0), (1, 0), (0, 0)))[:, :-1]
            return jnp.concatenate([a, s], -1)

        def l2norm(t):
            return t / jnp.maximum(jnp.linalg.norm(t, axis=-1, keepdims=True), 1e-12)

        def rotate_half(x):
            x1, x2 = jnp.split(x, 2, -1)
            return jnp.concatenate([-x2, x1], -1)

        def rotary_tables(n):
            half = jnp.arange(0, DIM_HEAD, 2, dtype=jnp.float32)
            inv_freq = 1.0 / 10000.0 ** (half / DIM_HEAD)
            t = jnp.arange(n, dtype=jnp.float32)
            freqs = t[:, None] * inv_freq[None, :]
            freqs = jnp.concatenate([freqs, freqs], -1)
            base_scale = (half + 0.4 * DIM_HEAD) / (1.4 * DIM_HEAD)
            power = (t - n // 2) / (WINDOW // 2)
            scale = base_scale[None, :] ** power[:, None]
            scale = jnp.concatenate([scale, scale], -1)
            return (freqs, scale)

        def local_attention(q, k, v):
            b, h, n, d = q.shape
            w = WINDOW
            nw = n // w
            bq = q.reshape(b, h, nw, w, d)
            bk = k.reshape(b, h, nw, w, d)
            bv = v.reshape(b, h, nw, w, d)

            def look(t):
                p = jnp.pad(t, ((0, 0), (0, 0), (1, 0), (0, 0), (0, 0)))
                return jnp.concatenate([p[:, :, :nw], p[:, :, 1:]], axis=3)
            bk2, bv2 = (look(bk), look(bv))
            seq = jnp.arange(n).reshape(nw, w)
            seq_p = jnp.pad(seq, ((1, 0), (0, 0)), constant_values=-1)
            jt = jnp.concatenate([seq_p[:nw], seq_p[1:]], axis=1)
            it = seq[:, :, None]
            jb = jt[:, None, :]
            mask = (it < jb) | (it > jb + w) | (jb == -1)
            sim = jnp.einsum('bhwie,bhwje->bhwij', bq, bk2) * QK_SCALE
            sim = jnp.where(mask, -jnp.finfo(sim.dtype).max, sim)
            attn = jax.nn.softmax(sim, -1)
            out = jnp.einsum('bhwij,bhwje->bhwie', attn, bv2)
            return out.reshape(b, h, n, d)

        def attn_layer(x, Wqkv, qs, ksc, Wo):
            b, n, _ = x.shape
            qkv = x @ Wqkv
            q, k, v = jnp.split(qkv, 3, -1)
            sh = lambda t: t.reshape(b, n, HEADS, DIM_HEAD).transpose(0, 2, 1, 3)
            q, k, v = (sh(q), sh(k), sh(v))
            q = l2norm(q) * qs
            k = l2norm(k) * ksc
            freqs, scale = rotary_tables(n)
            cos, sin = (jnp.cos(freqs), jnp.sin(freqs))
            q = q * cos * scale + rotate_half(q) * sin * scale
            inv = 1.0 / scale
            k = k * cos * inv + rotate_half(k) * sin * inv
            out = local_attention(q, k, v)
            out = out.transpose(0, 2, 1, 3).reshape(b, n, INNER)
            return out @ Wo

        def ffn_layer(x, g, bln, W1, b1, W2, b2):
            mu = x.mean(-1, keepdims=True)
            var = ((x - mu) ** 2).mean(-1, keepdims=True)
            xn = (x - mu) / jnp.sqrt(var + 1e-05) * g + bln
            hg = xn @ W1 + b1
            a, gate = jnp.split(hg, 2, -1)
            return a * jax.nn.gelu(gate, approximate=False) @ W2 + b2
        key = jax.random.key(seed)
        ks = jax.random.split(key, 8)
        B, N = (2, 256)
        init = lambda k, shape: jax.random.normal(k, shape, jnp.float32) * 0.02
        return {'x': jax.random.normal(ks[0], (B, N, DIM), jnp.float32), 'Wqkv': init(ks[1], (DEPTH, DIM, 3 * INNER)), 'q_scale': jnp.ones((DEPTH, DIM_HEAD), jnp.float32), 'k_scale': jnp.ones((DEPTH, DIM_HEAD), jnp.float32), 'Wo': init(ks[2], (DEPTH, INNER, DIM)), 'ln_g': jnp.ones((DEPTH, DIM), jnp.float32), 'ln_b': jnp.zeros((DEPTH, DIM), jnp.float32), 'W1': init(ks[3], (DEPTH, DIM, 2 * DIM_INNER)), 'b1': jnp.zeros((DEPTH, 2 * DIM_INNER), jnp.float32), 'W2': init(ks[4], (DEPTH, DIM_INNER, DIM)), 'b2': jnp.zeros((DEPTH, DIM), jnp.float32)}
    _L0_ffn_in = _L0_ffn_setup()

    def _L1_attn_setup():
        import jax, jax.numpy as jnp
        import numpy as np
        NUM_HEADS = 16

        def rotate_half(x):
            h = x.shape[-1] // 2
            return jnp.concatenate([-x[..., h:], x[..., :h]], axis=-1)
        key = jax.random.key(seed)
        ks = jax.random.split(key, 9)
        d = 128
        s = 0.02
        return {'x': jax.random.normal(ks[0], (4, 256, d), dtype=jnp.float32), 'wq': jax.random.normal(ks[1], (d, d), dtype=jnp.float32) * s, 'bq': jax.random.normal(ks[2], (d,), dtype=jnp.float32) * s, 'wk': jax.random.normal(ks[3], (d, d), dtype=jnp.float32) * s, 'bk': jax.random.normal(ks[4], (d,), dtype=jnp.float32) * s, 'wv': jax.random.normal(ks[5], (d, d), dtype=jnp.float32) * s, 'bv': jax.random.normal(ks[6], (d,), dtype=jnp.float32) * s, 'wo': jax.random.normal(ks[7], (d, d), dtype=jnp.float32) * s, 'bo': jax.random.normal(ks[8], (d,), dtype=jnp.float32) * s}
    _L1_attn_in = _L1_attn_setup()

    def _L1_ffn_setup():
        import jax, jax.numpy as jnp
        import numpy as np
        import math
        D_MODEL = 128
        N_EXPERTS = 16
        D_FF = 512
        CAP_FACTOR = 1.25
        MIN_CAPACITY = 4

        def _capacity(num_tokens, num_experts):
            cap = math.floor(CAP_FACTOR * num_tokens / num_experts)
            cap += cap % 2
            return max(cap, MIN_CAPACITY)

        def _top1_router(gate_logits, capacity):
            s, e = gate_logits.shape
            probs = jax.nn.softmax(gate_logits, axis=-1)
            top1 = jnp.argmax(gate_logits, axis=-1)
            mask = jax.nn.one_hot(top1, e, dtype=jnp.int32)
            ranks = jnp.cumsum(mask, axis=0) - 1
            mask = mask * (ranks < capacity).astype(jnp.int32)
            rank1 = jnp.sum(mask * ranks, axis=-1)
            ranks_oh = jax.nn.one_hot(rank1, capacity, dtype=probs.dtype)
            weight = mask.astype(probs.dtype) * probs
            combine_weights = weight[:, :, None] * ranks_oh[:, None, :]
            sec_mask = combine_weights > 0
            return (combine_weights, sec_mask)
        key = jax.random.key(seed)
        k1, k2, k3, k4 = jax.random.split(key, 4)
        x = jax.random.normal(k1, (4, 256, D_MODEL), dtype=jnp.float32)
        gate_w = jax.random.normal(k2, (N_EXPERTS, D_MODEL), dtype=jnp.float32) * math.sqrt(0.1 / D_MODEL)
        w1 = jax.random.normal(k3, (N_EXPERTS, D_MODEL, D_FF), dtype=jnp.float32) * (1.0 / math.sqrt(D_MODEL))
        w2 = jax.random.normal(k4, (N_EXPERTS, D_FF, D_MODEL), dtype=jnp.float32) * (1.0 / math.sqrt(D_FF))
        return {'x': x, 'gate_w': gate_w, 'w1': w1, 'w2': w2}
    _L1_ffn_in = _L1_ffn_setup()
    _d = {'L0_attn_x': _L0_attn_in['x'], 'L0_attn_Wd_q_w': _L0_attn_in['Wd_q_w'], 'L0_attn_Wd_q_b': _L0_attn_in['Wd_q_b'], 'L0_attn_Wu_q_w': _L0_attn_in['Wu_q_w'], 'L0_attn_Wu_q_b': _L0_attn_in['Wu_q_b'], 'L0_attn_Wq_r_w': _L0_attn_in['Wq_r_w'], 'L0_attn_Wq_r_b': _L0_attn_in['Wq_r_b'], 'L0_attn_Wk_r_w': _L0_attn_in['Wk_r_w'], 'L0_attn_Wk_r_b': _L0_attn_in['Wk_r_b'], 'L0_attn_Wd_kv_w': _L0_attn_in['Wd_kv_w'], 'L0_attn_Wd_kv_b': _L0_attn_in['Wd_kv_b'], 'L0_attn_Wu_k_w': _L0_attn_in['Wu_k_w'], 'L0_attn_Wu_k_b': _L0_attn_in['Wu_k_b'], 'L0_attn_Wu_v_w': _L0_attn_in['Wu_v_w'], 'L0_attn_Wu_v_b': _L0_attn_in['Wu_v_b'], 'L0_attn_Wo_w': _L0_attn_in['Wo_w'], 'L0_attn_Wo_b': _L0_attn_in['Wo_b'], 'L0_ffn_Wqkv': _L0_ffn_in['Wqkv'], 'L0_ffn_q_scale': _L0_ffn_in['q_scale'], 'L0_ffn_k_scale': _L0_ffn_in['k_scale'], 'L0_ffn_Wo': _L0_ffn_in['Wo'], 'L0_ffn_ln_g': _L0_ffn_in['ln_g'], 'L0_ffn_ln_b': _L0_ffn_in['ln_b'], 'L0_ffn_W1': _L0_ffn_in['W1'], 'L0_ffn_b1': _L0_ffn_in['b1'], 'L0_ffn_W2': _L0_ffn_in['W2'], 'L0_ffn_b2': _L0_ffn_in['b2'], 'L1_attn_wq': _L1_attn_in['wq'], 'L1_attn_bq': _L1_attn_in['bq'], 'L1_attn_wk': _L1_attn_in['wk'], 'L1_attn_bk': _L1_attn_in['bk'], 'L1_attn_wv': _L1_attn_in['wv'], 'L1_attn_bv': _L1_attn_in['bv'], 'L1_attn_wo': _L1_attn_in['wo'], 'L1_attn_bo': _L1_attn_in['bo'], 'L1_ffn_gate_w': _L1_ffn_in['gate_w'], 'L1_ffn_w1': _L1_ffn_in['w1'], 'L1_ffn_w2': _L1_ffn_in['w2']}
    _x0 = _d['L0_attn_x']
    _d['L0_attn_x'] = jax.random.normal(jax.random.fold_in(jax.random.key(seed), 1), (4, 512, 128), dtype=_x0.dtype)
    del _x0
    return _d

def reference(L0_attn_x, L0_attn_Wd_q_w, L0_attn_Wd_q_b, L0_attn_Wu_q_w, L0_attn_Wu_q_b, L0_attn_Wq_r_w, L0_attn_Wq_r_b, L0_attn_Wk_r_w, L0_attn_Wk_r_b, L0_attn_Wd_kv_w, L0_attn_Wd_kv_b, L0_attn_Wu_k_w, L0_attn_Wu_k_b, L0_attn_Wu_v_w, L0_attn_Wu_v_b, L0_attn_Wo_w, L0_attn_Wo_b, L0_ffn_Wqkv, L0_ffn_q_scale, L0_ffn_k_scale, L0_ffn_Wo, L0_ffn_ln_g, L0_ffn_ln_b, L0_ffn_W1, L0_ffn_b1, L0_ffn_W2, L0_ffn_b2, L1_attn_wq, L1_attn_bq, L1_attn_wk, L1_attn_bk, L1_attn_wv, L1_attn_bv, L1_attn_wo, L1_attn_bo, L1_ffn_gate_w, L1_ffn_w1, L1_ffn_w2):

    def _L0_attn_ref(x, Wd_q_w, Wd_q_b, Wu_q_w, Wu_q_b, Wq_r_w, Wq_r_b, Wk_r_w, Wk_r_b, Wd_kv_w, Wd_kv_b, Wu_k_w, Wu_k_b, Wu_v_w, Wu_v_b, Wo_w, Wo_b):
        import jax, jax.numpy as jnp
        import numpy as np
        NUM_HEAD = 16
        D_Q = 64
        D_KV = 64
        ROPE_BASE = 10000.0

        def _cos_sin(seq_len, dim):
            pos = jnp.arange(seq_len, dtype=jnp.float32)[:, None]
            ids = jnp.arange(dim // 2, dtype=jnp.float32)
            theta = ROPE_BASE ** (-2.0 * ids) / (dim // 2)
            r = pos * theta[None, :]
            return (jnp.cos(r), jnp.sin(r))

        def _rope(x, cos, sin):
            b, s, d = x.shape
            xv = x.reshape(b, s, d // 2, 2)
            x0, x1 = (xv[..., 0], xv[..., 1])
            out = jnp.stack([x0 * cos - x1 * sin, x1 * cos + x0 * sin], axis=-1)
            return out.reshape(b, s, d)
        b, s, d_model = x.shape
        h = NUM_HEAD
        hd = d_model // h
        scale = jnp.sqrt(jnp.float32(h + D_KV + D_Q))

        def heads(t):
            return t.reshape(b, s, h, hd).transpose(0, 2, 1, 3)
        cos, sin = _cos_sin(s, d_model)
        ct_q = x @ Wd_q_w + Wd_q_b
        qt_c = heads(ct_q @ Wu_q_w + Wu_q_b)
        qt_r = heads(_rope(ct_q @ Wq_r_w + Wq_r_b, cos, sin))
        query = qt_c + qt_r
        ct_kv = x @ Wd_kv_w + Wd_kv_b
        kt_c = heads(ct_kv @ Wu_k_w + Wu_k_b)
        kt_r = heads(_rope(x @ Wk_r_w + Wk_r_b, cos, sin))
        key = kt_c + kt_r
        value = heads(ct_kv @ Wu_v_w + Wu_v_b)
        attn = jnp.einsum('bhqd,bhkd->bhqk', query, key) / scale
        attn = jax.nn.softmax(attn, axis=-1)
        out = jnp.einsum('bhqk,bhkd->bhqd', attn, value)
        out = out.transpose(0, 2, 1, 3).reshape(b, s, d_model)
        return out @ Wo_w + Wo_b

    def _L0_ffn_ref(x, Wqkv, q_scale, k_scale, Wo, ln_g, ln_b, W1, b1, W2, b2):
        import jax, jax.numpy as jnp
        import numpy as np
        DIM = 128
        DEPTH = 6
        HEADS = 16
        DIM_HEAD = 64
        WINDOW = 32
        INNER = HEADS * DIM_HEAD
        DIM_INNER = int(DIM * 4 * 2 / 3)
        QK_SCALE = 8.0

        def shift_tokens(t):
            a, s = jnp.split(t, 2, -1)
            s = jnp.pad(s, ((0, 0), (1, 0), (0, 0)))[:, :-1]
            return jnp.concatenate([a, s], -1)

        def l2norm(t):
            return t / jnp.maximum(jnp.linalg.norm(t, axis=-1, keepdims=True), 1e-12)

        def rotate_half(x):
            x1, x2 = jnp.split(x, 2, -1)
            return jnp.concatenate([-x2, x1], -1)

        def rotary_tables(n):
            half = jnp.arange(0, DIM_HEAD, 2, dtype=jnp.float32)
            inv_freq = 1.0 / 10000.0 ** (half / DIM_HEAD)
            t = jnp.arange(n, dtype=jnp.float32)
            freqs = t[:, None] * inv_freq[None, :]
            freqs = jnp.concatenate([freqs, freqs], -1)
            base_scale = (half + 0.4 * DIM_HEAD) / (1.4 * DIM_HEAD)
            power = (t - n // 2) / (WINDOW // 2)
            scale = base_scale[None, :] ** power[:, None]
            scale = jnp.concatenate([scale, scale], -1)
            return (freqs, scale)

        def local_attention(q, k, v):
            b, h, n, d = q.shape
            w = WINDOW
            nw = n // w
            bq = q.reshape(b, h, nw, w, d)
            bk = k.reshape(b, h, nw, w, d)
            bv = v.reshape(b, h, nw, w, d)

            def look(t):
                p = jnp.pad(t, ((0, 0), (0, 0), (1, 0), (0, 0), (0, 0)))
                return jnp.concatenate([p[:, :, :nw], p[:, :, 1:]], axis=3)
            bk2, bv2 = (look(bk), look(bv))
            seq = jnp.arange(n).reshape(nw, w)
            seq_p = jnp.pad(seq, ((1, 0), (0, 0)), constant_values=-1)
            jt = jnp.concatenate([seq_p[:nw], seq_p[1:]], axis=1)
            it = seq[:, :, None]
            jb = jt[:, None, :]
            mask = (it < jb) | (it > jb + w) | (jb == -1)
            sim = jnp.einsum('bhwie,bhwje->bhwij', bq, bk2) * QK_SCALE
            sim = jnp.where(mask, -jnp.finfo(sim.dtype).max, sim)
            attn = jax.nn.softmax(sim, -1)
            out = jnp.einsum('bhwij,bhwje->bhwie', attn, bv2)
            return out.reshape(b, h, n, d)

        def attn_layer(x, Wqkv, qs, ksc, Wo):
            b, n, _ = x.shape
            qkv = x @ Wqkv
            q, k, v = jnp.split(qkv, 3, -1)
            sh = lambda t: t.reshape(b, n, HEADS, DIM_HEAD).transpose(0, 2, 1, 3)
            q, k, v = (sh(q), sh(k), sh(v))
            q = l2norm(q) * qs
            k = l2norm(k) * ksc
            freqs, scale = rotary_tables(n)
            cos, sin = (jnp.cos(freqs), jnp.sin(freqs))
            q = q * cos * scale + rotate_half(q) * sin * scale
            inv = 1.0 / scale
            k = k * cos * inv + rotate_half(k) * sin * inv
            out = local_attention(q, k, v)
            out = out.transpose(0, 2, 1, 3).reshape(b, n, INNER)
            return out @ Wo

        def ffn_layer(x, g, bln, W1, b1, W2, b2):
            mu = x.mean(-1, keepdims=True)
            var = ((x - mu) ** 2).mean(-1, keepdims=True)
            xn = (x - mu) / jnp.sqrt(var + 1e-05) * g + bln
            hg = xn @ W1 + b1
            a, gate = jnp.split(hg, 2, -1)
            return a * jax.nn.gelu(gate, approximate=False) @ W2 + b2
        for i in range(DEPTH):
            x = attn_layer(shift_tokens(x), Wqkv[i], q_scale[i], k_scale[i], Wo[i]) + x
            x = ffn_layer(shift_tokens(x), ln_g[i], ln_b[i], W1[i], b1[i], W2[i], b2[i]) + x
        return x

    def _L1_attn_ref(x, wq, bq, wk, bk, wv, bv, wo, bo):
        import jax, jax.numpy as jnp
        import numpy as np
        NUM_HEADS = 16

        def rotate_half(x):
            h = x.shape[-1] // 2
            return jnp.concatenate([-x[..., h:], x[..., :h]], axis=-1)
        b, s, d = x.shape
        h = NUM_HEADS
        hd = d // h
        q = x @ wq.T + bq
        k = x @ wk.T + bk
        v = x @ wv.T + bv
        q = q.reshape(b, s, h, hd).transpose(0, 2, 1, 3)
        k = k.reshape(b, s, h, hd).transpose(0, 2, 1, 3)
        v = v.reshape(b, s, h, hd).transpose(0, 2, 1, 3)
        theta = 10000.0 ** (-2.0 * jnp.arange(hd // 2, dtype=jnp.float32) / hd)
        freqs = jnp.arange(s, dtype=jnp.float32)[:, None] * theta[None, :]
        cos = jnp.repeat(jnp.cos(freqs), 2, axis=-1)[None, None]
        sin = jnp.repeat(jnp.sin(freqs), 2, axis=-1)[None, None]
        q = q * cos + rotate_half(q) * sin
        k = k * cos + rotate_half(k) * sin
        scores = jnp.einsum('bhqd,bhkd->bhqk', q, k) / jnp.sqrt(jnp.float32(hd))
        attn = jax.nn.softmax(scores, axis=-1)
        out = jnp.einsum('bhqk,bhkd->bhqd', attn, v)
        out = out.transpose(0, 2, 1, 3).reshape(b, s, d)
        return out @ wo.T + bo

    def _L1_ffn_ref(x, gate_w, w1, w2):
        import jax, jax.numpy as jnp
        import numpy as np
        import math
        D_MODEL = 128
        N_EXPERTS = 16
        D_FF = 512
        CAP_FACTOR = 1.25
        MIN_CAPACITY = 4

        def _capacity(num_tokens, num_experts):
            cap = math.floor(CAP_FACTOR * num_tokens / num_experts)
            cap += cap % 2
            return max(cap, MIN_CAPACITY)

        def _top1_router(gate_logits, capacity):
            s, e = gate_logits.shape
            probs = jax.nn.softmax(gate_logits, axis=-1)
            top1 = jnp.argmax(gate_logits, axis=-1)
            mask = jax.nn.one_hot(top1, e, dtype=jnp.int32)
            ranks = jnp.cumsum(mask, axis=0) - 1
            mask = mask * (ranks < capacity).astype(jnp.int32)
            rank1 = jnp.sum(mask * ranks, axis=-1)
            ranks_oh = jax.nn.one_hot(rank1, capacity, dtype=probs.dtype)
            weight = mask.astype(probs.dtype) * probs
            combine_weights = weight[:, :, None] * ranks_oh[:, None, :]
            sec_mask = combine_weights > 0
            return (combine_weights, sec_mask)
        tokens = x.reshape(-1, D_MODEL)
        s = tokens.shape[0]
        capacity = _capacity(s, N_EXPERTS)
        gate_logits = tokens.astype(jnp.float32) @ gate_w.T
        combine_weights, sec_mask = _top1_router(gate_logits, capacity)
        dispatch = jnp.einsum('sec,sd->ecd', sec_mask.astype(tokens.dtype), tokens)
        h = jax.nn.gelu(jnp.einsum('ecd,edf->ecf', dispatch, w1))
        expert_out = jnp.einsum('ecf,efd->ecd', h, w2)
        out = jnp.einsum('sec,ecd->sd', combine_weights.astype(tokens.dtype), expert_out)
        return out.reshape(x.shape)
    x = L0_attn_x
    x = x + _L0_attn_ref(_layernorm(x, axis=-1), L0_attn_Wd_q_w, L0_attn_Wd_q_b, L0_attn_Wu_q_w, L0_attn_Wu_q_b, L0_attn_Wq_r_w, L0_attn_Wq_r_b, L0_attn_Wk_r_w, L0_attn_Wk_r_b, L0_attn_Wd_kv_w, L0_attn_Wd_kv_b, L0_attn_Wu_k_w, L0_attn_Wu_k_b, L0_attn_Wu_v_w, L0_attn_Wu_v_b, L0_attn_Wo_w, L0_attn_Wo_b)
    x = x + _L0_ffn_ref(_layernorm(x, axis=-1), L0_ffn_Wqkv, L0_ffn_q_scale, L0_ffn_k_scale, L0_ffn_Wo, L0_ffn_ln_g, L0_ffn_ln_b, L0_ffn_W1, L0_ffn_b1, L0_ffn_W2, L0_ffn_b2)
    x = x + _L1_attn_ref(_layernorm(x, axis=-1), L1_attn_wq, L1_attn_bq, L1_attn_wk, L1_attn_bk, L1_attn_wv, L1_attn_bv, L1_attn_wo, L1_attn_bo)
    x = x + _L1_ffn_ref(_layernorm(x, axis=-1), L1_ffn_gate_w, L1_ffn_w1, L1_ffn_w2)
    return x

_drawn_inputs = setup_inputs


def setup_inputs(seed=0):
    import zlib

    import numpy as np

    out = dict(_drawn_inputs(seed))
    spreads = {'L0_attn_Wd_q_b': (0.0, 0.8),
     'L0_attn_Wu_q_b': (0.0, 0.8),
     'L0_attn_Wq_r_b': (0.0, 0.8),
     'L0_attn_Wk_r_b': (0.0, 2.0),
     'L0_attn_Wd_kv_b': (0.0, 0.8),
     'L0_attn_Wu_k_b': (0.0, 2.0),
     'L0_attn_Wu_v_b': (0.0, 0.347),
     'L0_attn_Wo_b': (0.0, 0.1),
     'L0_ffn_q_scale': (1.0, 0.6),
     'L0_ffn_k_scale': (1.0, 0.6),
     'L0_ffn_ln_g': (1.0, 0.6),
     'L0_ffn_ln_b': (0.0, 0.8),
     'L0_ffn_b1': (0.0, 0.8),
     'L0_ffn_b2': (0.0, 0.1)}
    factors = {'L0_attn_Wd_q_w': 8.0,
     'L0_attn_Wu_q_w': 8.0,
     'L0_attn_Wq_r_w': 8.0,
     'L0_attn_Wk_r_w': 8.0,
     'L0_attn_Wd_kv_w': 8.0,
     'L0_attn_Wu_k_w': 8.0,
     'L0_attn_Wu_v_w': 8.0,
     'L0_ffn_W1': 3.513,
     'L0_ffn_W2': 3.457,
     'L1_attn_wq': 8.0,
     'L1_attn_bq': 8.0,
     'L1_attn_wk': 8.0,
     'L1_attn_bk': 8.0,
     'L1_attn_wv': 8.0,
     'L1_attn_bv': 8.0,
     'L1_attn_wo': 8.0,
     'L1_attn_bo': 15.759,
     'L1_ffn_gate_w': 6.518,
     'L1_ffn_w1': 7.108,
     'L1_ffn_w2': 6.464}
    for name, (base, spread) in spreads.items():
        noise = np.random.default_rng([zlib.crc32(name.encode()), seed]).standard_normal(out[name].shape)
        drawn = base * np.exp(spread * noise) if base else spread * noise
        out[name] = jnp.asarray(drawn.astype(out[name].dtype))
    for name, factor in factors.items():
        out[name] = (out[name] * factor).astype(out[name].dtype)
    return out
```

```python
from contextlib import ExitStack

import concourse.bass as bass
from concourse import mybir
import numpy as np

F32 = mybir.dt.float32
BF16 = mybir.dt.bfloat16
U32 = mybir.dt.uint32
I32 = mybir.dt.int32
ALU = mybir.AluOpType
ACT = mybir.ActivationFunctionType
AX = mybir.AxisListType

P = 128
BATCH, SEQ = 4, 512
TILES = SEQ // P
TOKENS = BATCH * SEQ
NT = TOKENS // P
EPS = 1e-5
AH, AD = 16, 8
HG = 4
UNITS = TILES * HG
PAIRQ = 2 * UNITS
STACK = [(0, 0), (0, 1), (1, 0), (1, 1), (0, 2), (2, 0)]
STACK_ROW = [0, 8, 16, 24, 40, 48]
MAX_ROW = 32
AV = 32
DEPTH, LH, LD, WIN = 6, 16, 64, 32
PAIRS = LH // 2
INNER = LH * LD
FF = int(P * 4 * 2 / 3)
FCH = [(0, 128), (128, 128), (256, FF - 256)]
NEG = -1e30
SCALE = [float(np.sqrt(np.float32(AH + 64 + 64))), float(np.sqrt(np.float32(AD)))]
NE, DFF = 16, 512
CAP = 160
HC = CAP // 2
SLOTS = NE * CAP


class Chain:

    def __init__(self, eng, sem, start):
        self.eng, self.sem, self.value = eng, sem, start

    def link(self, ins):
        ins.then_inc(self.sem, 1)
        self.value = self.value + 1
        self.eng.wait_ge(self.sem, self.value)


def build(nc, I, out):
    with ExitStack() as ctx:
        def sb(name, shape, dt=F32):
            return ctx.enter_context(nc.sbuf_tensor(name, shape, dt))

        def sem(name):
            return ctx.enter_context(nc.semaphore(name))

        bank = ctx.enter_context(nc.psum_tensor("bank", [P, 8, 512], F32))

        xT = sb("xT", [P, BATCH, SEQ])
        zT = sb("zT", [P, BATCH, SEQ])
        ident = sb("ident", [P, P])
        mean_w = sb("mean_w", [P, P])
        upper = sb("upper", [P, P])
        ropeC = sb("ropeC", [P, 2, SEQ])
        ropeS = sb("ropeS", [P, 2, SEQ])
        onesrow = sb("onesrow", [P, 1])
        packed_q, packed_k, packed_m = sb("packed_q", [P, 3, 512]), sb("packed_k", [P, 3, 512]), sb("packed_m", [P, 256])
        sel_q, sel_k, sel_m = (packed_q[:, :, :].bitcast(BF16), packed_k[:, :, :].bitcast(BF16), packed_m[:, :].bitcast(BF16))
        rotC = sb("rotC", [P, TILES, 2 * LD])
        rotS = sb("rotS", [P, TILES, 2 * LD])
        maskw = sb("maskw", [P, 2, P], BF16)
        maskr = sb("maskr", [P, 512], BF16)
        moe_c = sb("moe_c", [P, 3, NE])
        wdq = sb("wdq", [P, 64])
        wdkv = sb("wdkv", [P, 64])
        wuq = sb("wuq", [64, P])
        wuk = sb("wuk", [64, P])
        wuv = sb("wuv", [64, P])
        wqr = sb("wqr", [64, 2, P])
        wkr = sb("wkr", [P, 2, P])
        wq1 = sb("wq1", [P, 2, P])
        wk1 = sb("wk1", [P, 2, P])
        wv1 = sb("wv1", [P, P])
        wo = sb("wo", [P, 2, P])
        bias = sb("bias", [P, 16])
        wqkv = sb("wqkv", [P, 3 * INNER])
        wol = sb("wol", [P, PAIRS, P])
        w1 = sb("w1", [P, 2 * FF])
        w2 = sb("w2", [P, 3, P])
        lb = sb("lb", [P, 10])
        qks = sb("qks", [P, 2, LD])
        rotCl = sb("rotCl", [P, TILES, 2 * LD])
        rotSl = sb("rotSl", [P, TILES, 2 * LD])
        xc = sb("xc", [P, SEQ])
        sqn = sb("sqn", [P, SEQ])
        xn = xc
        tick = sb("tick", [P, 1])
        eps = sb("eps", [P, 1])
        xs = sb("xs", [P, WIN + SEQ])
        xf = sb("xf", [P, SEQ])
        kD = sb("kD", [P, 2, PAIRS, 2, WIN + P])
        qT = sb("qT", [P, 2, PAIRS, P])
        vbuf = sb("vbuf", [P, 4096])
        vD = vbuf[:, :].rearrange("p (w c r d) -> p w c r d", w=4, c=PAIRS, r=2)
        v2 = vbuf[:, :].rearrange("p (b w t) -> p b w t", b=2, w=4)
        big = sb("big", [P, 4, 2048])
        rotA, qn, sq, rotB = (big[:, j, :] for j in range(4))
        sc = sb("sc", [P, 4, 1024])
        mask_f = sc[:, 0, 0:768]
        oTl = sb("oTl", [P, PAIRS, SEQ])
        small = sb("small", [P, 8, 32])
        gates = sb("gates", [P, 3, SEQ])
        rstd = gates[:, 2, :]
        hT = sb("hT", [P, 3, SEQ])
        cq, ckv = hT[0:64, 0, :], hT[0:64, 1, :]
        tA, tB = gates[:, 0, :], gates[:, 1, :]
        qf, kf = gates[:, 2, :], hT[:, 2, :]
        parts = big[:, 0, :].bitcast(BF16).rearrange("p (a t) -> p a t", t=SEQ)
        nmp = big[:, 1, 0:512].rearrange("p (q c) -> p q c", c=P)
        nm, nmr = (big[:, 1, c:c + 64].rearrange("p (q h) -> p q h", h=AH) for c in (512, 576))
        nmb = big[:, 1, 640:672].bitcast(BF16).rearrange("p (q h) -> p q h", h=AH)
        nmT = big[:, 1, 768:1024].bitcast(BF16)
        tC = big[:, 1, 1024:1536]
        pT = big[:, 2:4, :].rearrange("p b (g t) -> p b g t", g=HG)
        qst = oTl[:, :, :].bitcast(BF16).rearrange("p a (r t) -> p a r t", r=2)
        kst = vbuf[:, 0:2048].bitcast(BF16).rearrange("p (a t) -> p a t", t=SEQ)
        va = v2[:, 1, :, :].rearrange("p c (h e) -> p c h e", h=AH)
        oU = sc[:, 0:2, :].rearrange("p a (b t) -> p (a b) t", b=2)
        rinv = small[:, 0:2, :].rearrange("p a b -> p (a b)")
        on = sc[:, 3, 0:256].rearrange("p (b t) -> p b t", b=2)
        oT = sc[:, 3, 512:1024]
        ones = rotCl[:, 0, :]
        xtok = sc[:, 0:2, :].rearrange("p a (b d) -> p (a b) d", d=P)
        idx = sb("idx", [P, 2, NT], U32)
        rt = big[:, 1:3, :].rearrange("p a (b t) -> p (a b) t", t=256)
        rs = small
        ew1 = wqkv[:, 0:1024].rearrange("p (b f) -> p b f", b=2)
        ew2 = wqkv[:, 1024:2048].rearrange("p (b f d) -> p b f d", b=2, f=4)
        xd = oTl[0:HC, :, :].rearrange("p a (b d) -> p (a b) d", d=P)
        dT = v2[:, 0, 0:2, 0:CAP]
        eh = v2[:, 1, :, 0:2 * CAP].rearrange("p (a b) (c t) -> p a b c t", a=2, c=2)
        yo = big[0:HC, 0, 0:512].rearrange("p (a c d) -> p a c d", a=2, c=2)
        gat = qT[:, :, :, :].rearrange("p a b d -> p (a b) d")
        fin = big[:, 3, :].rearrange("p (a d) -> p a d", d=P)

        disp = nc.dram_tensor("dispatch_rows", (SLOTS + TOKENS, P), F32, kind="Internal").ap()
        yrow = nc.dram_tensor("expert_rows", (SLOTS, P), F32, kind="Internal").ap()

        ld_x, ld_c, ld_w = sem("ld_x"), sem("ld_c"), sem("ld_w")
        init, zeros_set, settled, masks_set = sem("init"), sem("zeros_set"), sem("settled"), sem("masks_set")
        x_tr, x_in = sem("x_tr"), sem("x_in")
        ln_mean, ln_c, ln_sq, ln_var, ln_r, ln_i, ln_out = (
            sem(n) for n in ("ln_mean", "ln_c", "ln_sq", "ln_var", "ln_r", "ln_i", "ln_out"))
        step_done = sem("step_done")
        a_lat, a_latc, a_q, a_k, a_v, a_vc = (sem(n) for n in ("a_lat", "a_latc", "a_q", "a_k", "a_v", "a_vc"))
        a_qf, a_kf, a_ch, a_ch1, a_rc = sem("a_qf"), sem("a_kf"), sem("a_ch"), sem("a_ch1"), sem("a_rc")
        a_sk, a_sq, a_ke, a_qe, a_qo, a_nm, a_tc, a_sm, a_me, a_mo = (
            sem(n) for n in ("a_sk", "a_sq", "a_ke", "a_qe", "a_qo", "a_nm", "a_tc", "a_sm", "a_me", "a_mo"))
        x_sum = sem("x_sum")
        a_clr, a_s, a_mx, a_t, a_st, a_p, a_pv, a_oc, a_ob = (
            sem(n) for n in ("a_clr", "a_s", "a_mx", "a_t", "a_st", "a_p", "a_pv", "a_oc", "a_ob"))
        a_on, a_ot, a_otc, a_wo = sem("a_on"), sem("a_ot"), sem("a_otc"), sem("a_wo")
        ld_qkv, ld_f = sem("ld_qkv"), sem("ld_f")
        l_chr, l_chs, l_tab, l_kh, l_trs = sem("l_chr"), sem("l_chs"), sem("l_tab"), sem("l_kh"), sem("l_trs")
        l_xs, l_qk, l_v, l_sq, l_vc, l_qn, l_rb = (
            sem(n) for n in ("l_xs", "l_qk", "l_v", "l_sq", "l_vc", "l_qn", "l_rb"))
        l_ra, l_yq, l_yk, l_tr, l_trc, l_s, l_e, l_p = (
            sem(n) for n in ("l_ra", "l_yq", "l_yk", "l_tr", "l_trc", "l_s", "l_e", "l_p"))
        l_pt, l_ptc, l_pv, l_on, l_ot, l_oc, l_wo, l_res, l_xf, l_fn = (
            sem(n) for n in ("l_pt", "l_ptc", "l_pv", "l_on", "l_ot", "l_oc", "l_wo", "l_res", "l_xf", "l_fn"))
        f_h, f_g, f_hd, f_y = sem("f_h"), sem("f_g"), sem("f_hd"), sem("f_y")
        m_lg, m_sh, m_ex, m_oh, m_cum, m_ch, m_idx = (
            sem(n) for n in ("m_lg", "m_sh", "m_ex", "m_oh", "m_cum", "m_ch", "m_idx"))
        m_tk, m_tkc, m_zero, m_sc, m_xd = (sem(n) for n in ("m_tk", "m_tkc", "m_zero", "m_sc", "m_xd"))
        m_w, m_yo = [[sem(f"{n}{j}") for j in range(2)] for n in ("m_w", "m_yo")]
        m_d, m_dc, m_h, m_hc, m_y, m_yc, m_g = (
            sem(n) for n in ("m_d", "m_dc", "m_h", "m_hc", "m_y", "m_yc", "m_g"))
        m_xo, m_fin, m_out = sem("m_xo"), sem("m_fin"), sem("m_out")

        block = ctx.enter_context(nc.Block())

        def settle(eng):
            eng.sem_inc(settled, 1)

        def ln_mean_of(pe, src, b0):
            pe.matmul(bank[:, b0, :], mean_w[:, :], src, start=True, stop=True).then_inc(ln_mean, 1)

        def ln_var_of(pe, k, b1):
            pe.wait_ge(ln_sq, k + 1)
            pe.matmul(bank[:, b1, :], mean_w[:, :], sqn[:, :], start=True, stop=True).then_inc(ln_var, 1)

        def ln_tensor(pe, k, src, b0, b1):
            ln_mean_of(pe, src, b0)
            ln_var_of(pe, k, b1)

        def ln_centre(dve, k, src, b0):
            dve.wait_ge(ln_mean, k + 1)
            dve.tensor_tensor(xc[:, :], src, bank[:, b0, :], ALU.subtract).then_inc(ln_c, 1)

        def ln_scale(dve, k, dst):
            dve.wait_ge(ln_r, k + 1)
            dve.reciprocal(sqn[:, :], rstd[:, :]).then_inc(ln_i, 1)
            dve.wait_ge(ln_i, k + 1)
            dve.tensor_tensor(dst, xc[:, :], sqn[:, :], ALU.mult).then_inc(ln_out, 1)

        def ln_vector(dve, k, src, dst, b0, b1):
            ln_centre(dve, k, src, b0)
            ln_scale(dve, k, dst)

        def ln_scalar(act, k, b1):
            act.wait_ge(ln_c, k + 1)
            act.activation(sqn[:, :], xc[:, :], ACT.Square).then_inc(ln_sq, 1)
            act.wait_ge(ln_var, k + 1)
            act.activation(rstd[:, :], bank[:, b1, :], ACT.Sqrt, bias=eps[:, 0:1]).then_inc(ln_r, 1)

        const_loads = [
            (mean_w[:, :], I["c_mean"]), (ropeC[:, :, :], I["c_ropeC"]), (ropeS[:, :, :], I["c_ropeS"]),
            (onesrow[:, :], I["c_onesrow"]),
            (packed_q[:, :, :], I["c_selq"]), (packed_k[:, :, :], I["c_selk"]), (packed_m[:, :], I["c_selm"]), (rotC[:, :, :], I["c_rotC"]), (rotS[:, :, :], I["c_rotS"]),
            (mask_f[:, 0:256], I["c_maskw"]), (mask_f[:, 256:768], I["c_maskr"]), (moe_c[:, :, :], I["c_moe"]),
            (upper[:, :], I["c_upper"]),
        ]

        def col(name):
            return I[name].rearrange("(p o) -> p o", o=1)

        gw = sb("gw", [P, NE])
        weight_loads = [
            (wdq[:, :], I["L0_attn_Wd_q_w"]), (wdkv[:, :], I["L0_attn_Wd_kv_w"]),
            (wuq[:, :], I["L0_attn_Wu_q_w"]), (wuk[:, :], I["L0_attn_Wu_k_w"]), (wuv[:, :], I["L0_attn_Wu_v_w"]),
            (wqr[:, 0, :], I["L0_attn_Wq_r_w"]), (wqr[:, 1, :], I["wqr_swapped"]),
            (wkr[:, 0, :], I["L0_attn_Wk_r_w"]), (wkr[:, 1, :], I["wkr_swapped"]),
            (wo[:, 0, :], I["L0_attn_Wo_w"]), (wo[:, 1, :], I["wo_t"]),
            (wq1[:, 0, :], I["wq_t"]), (wq1[:, 1, :], I["wq_swapped"]),
            (wk1[:, 0, :], I["wk_t"]), (wk1[:, 1, :], I["wk_swapped"]), (wv1[:, :], I["wv_t"]),
            (bias[0:64, 0:1], col("L0_attn_Wd_q_b")), (bias[0:64, 1:2], col("L0_attn_Wd_kv_b")),
            (bias[:, 2:3], col("L0_attn_Wu_q_b")), (bias[:, 3:4], col("L0_attn_Wu_k_b")),
            (bias[:, 4:5], col("L0_attn_Wq_r_b")), (bias[:, 5:6], col("bqr_swapped")),
            (bias[:, 6:7], col("L0_attn_Wk_r_b")), (bias[:, 7:8], col("bkr_swapped")),
            (bias[:, 8:9], col("L0_attn_Wu_v_b")), (bias[:, 9:10], col("L0_attn_Wo_b")),
            (bias[:, 10:11], col("L1_attn_bq")), (bias[:, 11:12], col("bq_swapped")),
            (bias[:, 12:13], col("L1_attn_bk")), (bias[:, 13:14], col("bk_swapped")),
            (bias[:, 14:15], col("L1_attn_bv")), (bias[:, 15:16], col("L1_attn_bo")),
            (gw[:, :], I["gate_t"]),
        ]
        xrows = I["L0_attn_x"].rearrange("a (c p) d -> p (a c) d", p=P)
        LOADED = 16 * (len(const_loads) + len(weight_loads))
        SEED, LAYER0, ATT1, MOE0 = BATCH, 2 * BATCH, (2 + DEPTH) * BATCH, (3 + DEPTH) * BATCH
        LDQ, LDF = 3 * 16, 13 * 16

        @block.sync
        def _(sp):
            sp.dma_start(ident[:, :], I["c_ident"]).then_inc(ld_x, 16)
            sp.dma_start(big[:, 0, :].rearrange("p (a d) -> p a d", d=P), xrows).then_inc(ld_x, 16)
            for dst, src in const_loads + weight_loads:
                sp.dma_start(dst, src).then_inc(ld_c, 16)
            sp.wait_ge(zeros_set, 1)
            for j in range(5):
                sp.dma_start(disp[j * 512:(j + 1) * 512, :].rearrange("(p r) d -> p (r d)", r=4),
                             oTl[:, 0, :]).then_inc(m_zero, 16)
            def load_layer(l, first):
                if not first:
                    sp.wait_ge(l_v, l * (4 * TILES * BATCH))
                    settle(sp)
                    sp.wait_ge(l_qk, l * (TILES * BATCH))
                    settle(sp)
                sp.dma_start(wqkv[:, :], I["L0_ffn_Wqkv"][l, :, :]).then_inc(ld_qkv, 16)
                if not first:
                    sp.wait_ge(l_tab, l * 3)
                    settle(sp)
                for j, name in enumerate(("L0_ffn_q_scale", "L0_ffn_k_scale")):
                    sp.dma_start(qks[:, j, :], I[name][l, :].rearrange("(o d) -> o d", o=1).broadcast_to([P, LD])).then_inc(ld_qkv, 16)
                if not first:
                    sp.wait_ge(l_wo, l * BATCH)
                sp.dma_start(wol[:, :, :], I["L0_ffn_Wo"][l, :, :].rearrange("(a p) d -> p a d", p=P)).then_inc(ld_f, 16)
                if not first:
                    sp.wait_ge(step_done, l * BATCH + LAYER0 + 1)
                sp.dma_start(w1[:, :], I["L0_ffn_W1"][l, :, :]).then_inc(ld_f, 16)
                sp.dma_start(w2[:, 0:2, :], I["L0_ffn_W2"][l, 0:256, :].rearrange("(a p) d -> p a d", p=P)).then_inc(ld_f, 16)
                sp.dma_start(w2[0:FCH[2][1], 2, :], I["L0_ffn_W2"][l, 256:FF, :]).then_inc(ld_f, 16)
                for j, name in enumerate(("L0_ffn_ln_g", "L0_ffn_ln_b", "L0_ffn_b2")):
                    sp.dma_start(lb[:, j:j + 1], I[name][l, :].rearrange("(p o) -> p o", o=1)).then_inc(ld_f, 16)
                for j in range(6):
                    c0, n = FCH[j % 3]
                    c0 += FF * (j // 3)
                    sp.dma_start(lb[0:n, 3 + j:4 + j], I["L0_ffn_b1"][l, c0:c0 + n].rearrange("(p o) -> p o", o=1)).then_inc(ld_f, 16)

            load_layer(0, True)
            with sp.Fori(1, DEPTH) as l:
                load_layer(l, False)
            sp.wait_ge(step_done, ATT1 + 1)
            for e in range(NE):
                if e >= 2:
                    sp.wait_ge(m_h, e - 1)
                    sp.wait_ge(m_y, e - 1)
                sp.dma_start(ew1[:, e % 2, :], I["L1_ffn_w1"][e]).then_inc(m_w[e % 2], 16)
                sp.dma_start(ew2[:, e % 2, :, :], I["L1_ffn_w2"][e].rearrange("(f p) d -> p f d", p=P)).then_inc(m_w[e % 2], 16)
            sp.wait_ge(m_fin, 4)
            sp.dma_start(out.rearrange("a (c p) d -> p (a c) d", p=P), fin).then_inc(m_out, 16)
            sp.wait_ge(m_out, 16)

        @block.gpsimd
        def _(pool):
            pool.memset(oTl[:, :, :], 0.0).then_inc(zeros_set, 1)
            pool.memset(xs[:, 0:WIN + 1], 0.0).then_inc(init, 1)
            pool.memset(xf[:, 0:1], 0.0).then_inc(init, 1)
            pool.memset(kD[:, 0, :, :, :], 0.0).then_inc(init, 1)
            pool.memset(kD[:, 1, :, :, :], 0.0).then_inc(init, 1)
            pool.memset(eps[:, :], EPS).then_inc(init, 1)
            def clear():
                pool.memset(nmp, 0.0).then_inc(a_clr, 1)
                pool.memset(va[:, :, :, AD + 1:], 0.0).then_inc(a_clr, 1)
                pool.memset(va[:, :, :, AD:AD + 1], 1.0).then_inc(a_clr, 1)

            clear()
            pool.wait_ge(step_done, LAYER0 + 1)
            pool.memset(vbuf[:, :], 0.0).then_inc(zeros_set, 1)
            pool.sem_inc(l_trs, 1)
            with pool.Fori(0, DEPTH) as l:
                pool.wait_ge(l_tab, l * 3 + 3)
                settle(pool)
                with pool.Fori(0, BATCH) as b:
                    for i in range(TILES):
                        T = (l * BATCH + b) * TILES + i
                        pool.wait_ge(l_qn, T + 1)
                        pool.wait_ge(l_trs, T + 1)
                        q4 = qn.rearrange("p (a h d) -> p a h d", a=2, h=LH)
                        r4 = rotB.rearrange("p (a h d) -> p a h d", a=2, h=LH)
                        tab = rotSl[:, i, :].rearrange("p (a d) -> p a d", a=2).unsqueeze(2).broadcast_to([P, 2, LH, LD])
                        h = LD // 2
                        pool.tensor_tensor(r4[:, :, :, 0:h], q4[:, :, :, h:], tab[:, :, :, 0:h], ALU.mult).then_inc(l_rb, 1)
                        pool.tensor_tensor(r4[:, :, :, h:], q4[:, :, :, 0:h], tab[:, :, :, h:], ALU.mult).then_inc(l_rb, 1)
                        pool.wait_ge(l_ra, T + 1)
                        pool.wait_ge(l_rb, 2 * T + 2)
                        pool.tensor_tensor(rotB[:, INNER:], rotA[:, INNER:], rotB[:, INNER:], ALU.add).then_inc(l_yk, 1)
                        if i + 1 < TILES:
                            pool.wait_ge(l_trc, 3 * T + 3)
                            settle(pool)
                            pool.tensor_copy(kD[:, (i + 1) % 2, :, :, 0:WIN], kD[:, i % 2, :, :, P:P + WIN]).then_inc(l_kh, 1)
            pool.wait_ge(step_done, ATT1 + 1)
            pool.memset(oTl[:, :, :], 0.0).then_inc(zeros_set, 1)
            pool.memset(ones, 1.0).then_inc(zeros_set, 1)
            clear()
            pool.wait_ge(m_zero, 5 * 16)
            pool.wait_ge(m_idx, 2)
            pool.wait_ge(m_tkc, 4)
            for i in range(NT):
                pool.indirect_dma_start(disp, bass.IndirectOffsetOnAxis(ap=idx[:, 0, i:i + 1], axis=0),
                                        xtok[:, i, :], None).then_inc(m_sc, 16)
            pool.wait_ge(m_sc, 16 * NT)
            pool.dma_start(xd, disp[0:SLOTS, :].rearrange("(a p) d -> p a d", p=HC)).then_inc(m_xd, 16)
            for e in range(NE):
                pool.wait_ge(m_yc, e + 1)
                pool.dma_start(yrow[e * CAP:(e + 1) * CAP, :].rearrange("(c p) d -> p c d", p=HC),
                               yo[:, e % 2, :, :]).then_inc(m_yo[e % 2], 16)
            for j in range(2):
                pool.wait_ge(m_yo[j], 16 * NE // 2)
            for i in range(NT):
                pool.indirect_dma_start(gat[:, i, :], None, yrow,
                                        bass.IndirectOffsetOnAxis(ap=idx[:, 1, i:i + 1], axis=0)).then_inc(m_g, 16)

        @block.tensor
        def _(pe):
            pe.wait_ge(ld_x, 32)
            xin = big[:, 0, :].rearrange("p (a d) -> p a d", d=P)
            for b in range(BATCH):
                for c in range(TILES):
                    t = pe.transpose(bank[:, b, c * P:(c + 1) * P], xin[:, b * TILES + c, :], ident[:, :])
                t.then_inc(x_tr, 1)
            pe.wait_ge(ld_c, LOADED)
            pe.wait_ge(x_in, BATCH)

            def attention(a):
                base = ATT1 if a else 0
                with pe.Fori(0, BATCH) as b:
                    k, n = base + b, a * BATCH + b
                    pe.wait_ge(step_done, k + 1)
                    ln_tensor(pe, k, xT[:, b, :], 0, 1)
                    pe.wait_ge(ln_out, k + 1)
                    if a == 0:
                        pe.matmul(bank[0:64, 2, :], wdq[:, :], xn[:, :], start=True, stop=True).then_inc(a_lat, 1)
                        pe.matmul(bank[0:64, 3, :], wdkv[:, :], xn[:, :], start=True, stop=True).then_inc(a_lat, 1)
                        pe.wait_ge(a_latc, 2 * n + 1)
                        pe.matmul(bank[:, 4, :], wuq[:, :], cq, start=True, stop=True)
                        pe.matmul(bank[:, 5, :], wqr[:, 0, :], cq, start=True, stop=True)
                        pe.matmul(bank[:, 6, :], wqr[:, 1, :], cq, start=True, stop=True).then_inc(a_q, 1)
                        pe.wait_ge(a_latc, 2 * n + 2)
                        pe.matmul(bank[:, 7, :], wuk[:, :], ckv, start=True, stop=True)
                        pe.matmul(bank[:, 2, :], wkr[:, 0, :], xn[:, :], start=True, stop=True)
                        pe.matmul(bank[:, 3, :], wkr[:, 1, :], xn[:, :], start=True, stop=True).then_inc(a_k, 1)
                        for c in range(TILES):
                            m = pe.matmul(bank[:, 0, c * P:(c + 1) * P], ckv[:, c * P:(c + 1) * P], wuv[:, :],
                                          start=True, stop=True)
                        m.then_inc(a_v, 1)
                    else:
                        pe.matmul(bank[:, 5, :], wq1[:, 0, :], xn[:, :], start=True, stop=True)
                        pe.matmul(bank[:, 6, :], wq1[:, 1, :], xn[:, :], start=True, stop=True).then_inc(a_q, 1)
                        pe.matmul(bank[:, 2, :], wk1[:, 0, :], xn[:, :], start=True, stop=True)
                        pe.matmul(bank[:, 3, :], wk1[:, 1, :], xn[:, :], start=True, stop=True).then_inc(a_k, 1)
                        for c in range(TILES):
                            m = pe.matmul(bank[:, 0, c * P:(c + 1) * P], xn[:, c * P:(c + 1) * P], wv1[:, :],
                                          start=True, stop=True)
                        m.then_inc(a_v, 1)
                    pe.wait_ge(a_qf, 3 * (n + 1))
                    pe.wait_ge(a_kf, 3 * (n + 1))
                    pe.wait_ge(a_vc, n + 1)

                    for half in range(2):
                        for p in range(4 * half, 4 * half + 4):
                            for part in range(3):
                                m = pe.matmul(bank[:, p, :], sel_k[:, part, p * P:(p + 1) * P], parts[:, 3 + part, :],
                                              start=(part == 0), stop=(part == 2))
                        m.then_inc(a_sk, 1)
                    for half in range(2):
                        pe.wait_ge(a_ke, 2 * n + half + 1)
                        for p in range(4 * half, 4 * half + 4):
                            for part in range(3):
                                for r in range(2):
                                    m = pe.matmul(bank[64 * r:64 * r + 64, p, :], sel_q[:, part, p * P + 64 * r:p * P + 64 * r + 64],
                                                  parts[:, part, :], start=(part == 0), stop=(part == 2), skip_group_check=True)
                        m.then_inc(a_sq, 1)

                    for u in range(UNITS):
                        qt, j = divmod(u, HG)
                        if u < 2:
                            pe.wait_ge(a_qe, 2 * n + u + 1)
                            pe.wait_ge(a_qo, 2 * n + u + 1)
                        else:
                            pe.wait_ge(a_mx, n * UNITS + u - 1)
                        for g in range(4):
                            h = 4 * j + g
                            m = pe.matmul(bank[:, 4 * (u % 2) + g, :], qst[:, h // 2, h % 2, qt * P:(qt + 1) * P],
                                          kst[:, h // 2, :], start=True, stop=True)
                        m.then_inc(a_s, 1)
                    pe.wait_ge(a_nm, n + 1)
                    for qt in range(TILES):
                        t = pe.transpose(bank[:, 0, qt * P:(qt + 1) * P], nmp[:, qt, :], ident[:, :])
                    t.then_inc(a_t, 1)
                    pe.wait_ge(a_tc, n + 1)
                    for half in range(2):
                        for p in range(4 * half, 4 * half + 4):
                            for r in range(2):
                                h = 2 * p + r
                                m = pe.matmul(bank[64 * r + MAX_ROW:64 * r + MAX_ROW + 32, p, :], sel_m[:, 32 * h:32 * h + 32], nmT,
                                              start=True, stop=True, tile_position=(0, 64 * r + MAX_ROW), skip_group_check=True)
                        m.then_inc(a_sm, 1)
                    pe.wait_ge(a_me, 2 * (n + 1))
                    pe.wait_ge(a_mo, 2 * (n + 1))

                    def scores_t(i):
                        u, half = divmod(i, 2)
                        j, kt = divmod(u, TILES)
                        if i >= 3:
                            pe.wait_ge(a_p, n * PAIRQ + i - 2)
                        for r in range(2):
                            m = pe.matmul(bank[:, 2 * (i % 3) + r, :], kst[:, 2 * j + half, kt * P:(kt + 1) * P],
                                          qst[:, 2 * j + half, r, :], start=True, stop=True)
                        m.then_inc(a_st, 1)

                    scores_t(0)
                    scores_t(1)
                    for u in range(UNITS):
                        if u + 1 < UNITS:
                            scores_t(2 * u + 2)
                            scores_t(2 * u + 3)
                        j, kt = divmod(u, TILES)
                        pe.wait_ge(a_p, n * PAIRQ + 2 * u + 2)
                        if kt == 0 and j >= 2:
                            pe.wait_ge(a_oc, n * HG + j - 1)
                        for g in range(4):
                            m = pe.matmul(bank[32 * g:32 * g + AV, 6 + j % 2, :], va[:, kt, HG * j + g, :],
                                          pT[:, u % 2, g, :], start=(kt == 0), stop=(kt == TILES - 1),
                                          tile_position=(0, 32 * g))
                        m.then_inc(a_pv, 1)
                    pe.wait_ge(a_oc, HG * (n + 1))
                    for qt in range(TILES):
                        for j in range(HG):
                            t = pe.transpose(bank[:, qt, j * P:(j + 1) * P], oU[:, j, qt * P:(qt + 1) * P], ident[:, :])
                        t.then_inc(a_ob, 1)
                    for qt in range(TILES):
                        pe.wait_ge(a_on, n * TILES + qt + 1)
                        pe.transpose(bank[:, 4, qt * P:(qt + 1) * P], on[:, qt % 2, :], ident[:, :]).then_inc(a_ot, 1)
                    pe.wait_ge(a_otc, n + 1)
                    pe.matmul(bank[:, 5, :], wo[:, a, :], oT, start=True, stop=True).then_inc(a_wo, 1)

            attention(0)

            with pe.Fori(0, BATCH) as b:
                k = SEED + b
                pe.wait_ge(step_done, k + 1)
                ln_tensor(pe, k, xT[:, b, :], 0, 1)

            def tiles(l, b, tail):
                it = l * BATCH + b

                def project_qk(i):
                    T = it * TILES + i
                    if i >= 1 or tail:
                        pe.wait_ge(l_qn, T)
                    if tail and i == 3:
                        pe.wait_ge(f_hd, 3 * it - 1)
                    for c in range(4):
                        m = pe.matmul(bank[:, c, :], xs[:, WIN + i * P:WIN + (i + 1) * P],
                                      wqkv[:, c * 512:(c + 1) * 512], start=True, stop=True)
                    m.then_inc(l_qk, 1)

                def project_v(i):
                    T = it * TILES + i
                    wv = wqkv[:, 2 * INNER:].rearrange("p (a r d) -> p r a d", r=2, d=LD)
                    if i >= 1:
                        pe.wait_ge(l_ptc, T)
                    for w in range(4):
                        if w >= 2:
                            pe.wait_ge(l_vc, 8 * T + 2 * (w - 1))
                        s = i * P + w * WIN
                        for r in range(2):
                            m = pe.matmul(bank[64 * r:64 * r + 64, 6 + w % 2, :], xs[:, s:s + 2 * WIN],
                                          wv[:, r, :, :], start=True, stop=True)
                        m.then_inc(l_v, 1)

                def turn_qk(i):
                    T = it * TILES + i
                    if i >= 1:
                        pe.wait_ge(l_on, T)
                    elif tail:
                        pe.wait_ge(ln_r, LAYER0 + it)
                        pe.wait_ge(ln_c, LAYER0 + it)
                    pe.wait_ge(l_yq, T + 1)
                    for c in range(PAIRS):
                        t = pe.transpose(bank[:, 4 + c // 4, (c % 4) * P:(c % 4 + 1) * P], rotB[:, c * P:(c + 1) * P], ident[:, :])
                    t.then_inc(l_tr, 1)
                    if i >= 1:
                        pe.wait_ge(l_oc, T)
                    else:
                        pe.wait_ge(l_vc, 8 * T + 8)
                    pe.wait_ge(l_yk, T + 1)
                    for c in range(PAIRS):
                        t = pe.transpose(bank[:, 6 + c // 4, (c % 4) * P:(c % 4 + 1) * P],
                                         rotB[:, INNER + c * P:INNER + (c + 1) * P], ident[:, :])
                    t.then_inc(l_tr, 1)
                    pe.sem_inc(l_trs, 1)

                def scores(i):
                    T = it * TILES + i
                    pe.wait_ge(l_trc, 3 * T + 1)
                    settle(pe)
                    for a in range(2):
                        pe.matmul(bank[:, 4 + a, :], maskw[:, min(i, 1), :], maskr[:, :], start=True, stop=False,
                                  skip_group_check=True)
                    pe.wait_ge(l_trc, 3 * T + 3)
                    if i >= 1:
                        pe.wait_ge(l_kh, it * (TILES - 1) + i)
                    settle(pe)
                    for c in range(PAIRS):
                        for w in range(4):
                            m = pe.matmul(bank[32 * w:32 * w + 32, 4 + c // 4, (c % 4) * P:(c % 4 + 1) * P],
                                          qT[:, i % 2, c, w * WIN:(w + 1) * WIN],
                                          kD[:, i % 2, c, :, w * WIN:(w + 2) * WIN], start=False, stop=True,
                                          tile_position=(0, 32 * w), skip_group_check=True)
                    m.then_inc(l_s, 1)

                def turn_p(i):
                    T = it * TILES + i
                    pe.wait_ge(l_p, T + 1)
                    for c in range(PAIRS):
                        t = pe.transpose(bank[:, 6 + c // 4, (c % 4) * P:(c % 4 + 1) * P], sc[:, 1, c * P:(c + 1) * P], ident[:, :])
                    t.then_inc(l_pt, 1)

                def weigh(i):
                    T = it * TILES + i
                    pe.wait_ge(l_vc, 8 * T + 8)
                    pe.wait_ge(l_ptc, T + 1)
                    pe.wait_ge(l_e, T + 1)
                    settle(pe)
                    for c in range(PAIRS):
                        for w in range(4):
                            m = pe.matmul(bank[32 * w:32 * w + 32, 4 + c // 4, (c % 4) * P:(c % 4 + 1) * P],
                                          sc[:, 3, c * P + w * WIN:c * P + (w + 1) * WIN], vD[:, w, c, :, :],
                                          start=True, stop=True, tile_position=(0, 32 * w))
                    m.then_inc(l_pv, 1)

                def turn_o(i):
                    T = it * TILES + i
                    pe.wait_ge(l_on, T + 1)
                    if i + 1 < TILES:
                        pe.wait_ge(l_vc, 8 * T + 16)
                    else:
                        pe.wait_ge(l_ptc, T + 1)
                    for c in range(PAIRS):
                        t = pe.transpose(bank[:, 6 + c // 4, (c % 4) * P:(c % 4 + 1) * P], sc[:, 2, c * P:(c + 1) * P], ident[:, :])
                    t.then_inc(l_ot, 1)

                pe.wait_ge(l_xs, 2 * it + 2)
                if tail:
                    pe.wait_ge(step_done, LAYER0 + it)
                project_qk(0)
                if tail:
                    project_out(it - 1)
                project_v(0)
                if tail:
                    ffn_mean(it - 1)
                project_qk(1)
                if tail:
                    ffn_var(it - 1)
                for i in range(TILES):
                    turn_qk(i)
                    if tail and i >= 1:
                        pe.wait_ge(l_qn, it * TILES + min(i + 2, TILES))
                        (ffn_in, ffn_in_last, ffn_out)[i - 1](it - 1)
                    scores(i)
                    if i + 2 < TILES:
                        project_qk(i + 2)
                    turn_p(i)
                    weigh(i)
                    if i + 1 < TILES:
                        project_v(i + 1)
                    turn_o(i)

            def project_out(it):
                pe.wait_ge(l_oc, (it + 1) * TILES)
                for c in range(PAIRS):
                    m = pe.matmul(bank[:, 4, :], wol[:, c, :], oTl[:, c, :], start=(c == 0), stop=(c == PAIRS - 1))
                m.then_inc(l_wo, 1)

            def ffn_mean(it):
                pe.wait_ge(l_xf, 2 * it + 2)
                ln_mean_of(pe, xf[:, :], 5)

            def ffn_var(it):
                ln_var_of(pe, LAYER0 + it, 4)

            def ffn_in(it):
                pe.wait_ge(l_fn, it + 1)
                for j in range(2):
                    c0, n = FCH[j]
                    pe.matmul(bank[0:n, 2 * j, :], w1[:, FF + c0:FF + c0 + n], xn[:, :], start=True, stop=True).then_inc(f_h, 1)
                    pe.matmul(bank[0:n, 2 * j + 1, :], w1[:, c0:c0 + n], xn[:, :], start=True, stop=True).then_inc(f_h, 1)

            def ffn_in_last(it):
                c0, n = FCH[2]
                pe.wait_ge(f_hd, 3 * it + 1)
                pe.matmul(bank[0:n, 0, :], w1[:, FF + c0:FF + c0 + n], xn[:, :], start=True, stop=True).then_inc(f_h, 1)
                pe.matmul(bank[0:n, 1, :], w1[:, c0:c0 + n], xn[:, :], start=True, stop=True).then_inc(f_h, 1)

            def ffn_out(it):
                for j in range(3):
                    pe.wait_ge(f_hd, 3 * it + max(j, 1) + 1)
                    n = FCH[j][1]
                    m = pe.matmul(bank[:, 2, :], w2[0:n, j, :], hT[0:n, j, :], start=(j == 0), stop=(j == 2))
                m.then_inc(f_y, 1)

            with pe.Fori(0, DEPTH) as l:
                pe.wait_ge(ld_qkv, l * LDQ + LDQ)
                pe.wait_ge(zeros_set, 2)
                pe.wait_ge(step_done, l * BATCH + LAYER0 + 1)
                settle(pe)
                tiles(l, 0, False)
                pe.wait_ge(ld_f, l * LDF + LDF)
                settle(pe)
                with pe.Fori(1, BATCH) as b:
                    tiles(l, b, True)
                last = l * BATCH + BATCH - 1
                project_out(last)
                ffn_mean(last)
                ffn_var(last)
                ffn_in(last)
                ffn_in_last(last)
                ffn_out(last)

            pe.wait_ge(x_sum, BATCH)
            attention(1)

            with pe.Fori(0, BATCH) as b:
                k = MOE0 + b
                pe.wait_ge(step_done, k + 1)
                ln_tensor(pe, k, xT[:, b, :], 0, 1)
            pe.wait_ge(step_done, MOE0 + BATCH + 1)
            zf = zT[:, :, :].rearrange("p b t -> p (b t)")
            for i in range(NT):
                m = pe.matmul(bank[:, 2, i * NE:(i + 1) * NE], zf[:, i * P:(i + 1) * P], gw[:, :], start=True, stop=True)
            m.then_inc(m_lg, 1)
            for i in range(NT):
                t = pe.transpose(bank[:, 3 + i // 4, (i % 4) * P:(i % 4 + 1) * P], zf[:, i * P:(i + 1) * P], ident[:, :])
            t.then_inc(m_tk, 1)
            pe.wait_ge(m_oh, 1)
            pe.wait_ge(zeros_set, 4)
            pe.matmul(bank[:, 7, 0:256], upper[:, :], rt[:, 3, :], start=True, stop=True)
            pe.matmul(bank[:, 0, 0:256], ones, rt[:, 3, :], start=True, stop=True).then_inc(m_cum, 1)
            pe.wait_ge(m_idx, 2)
            pe.wait_ge(m_tkc, 4)
            pe.wait_ge(m_xd, 16)

            def bring(e):
                if e >= 2:
                    pe.wait_ge(m_dc, e - 1)
                for c in range(2):
                    t = pe.transpose(bank[:, e % 2, c * HC:(c + 1) * HC], xd[:, 2 * e + c, :], ident[0:HC, 0:HC])
                t.then_inc(m_d, 1)

            bring(0)
            for e in range(NE):
                if e + 1 < NE:
                    bring(e + 1)
                pe.wait_ge(m_dc, e + 1)
                pe.wait_ge(m_w[e % 2], 32 * (e // 2 + 1))
                if e >= 1:
                    pe.wait_ge(m_hc, 2 * e)
                for f in range(4):
                    m = pe.matmul(bank[:, 2 + f // 2, (f % 2) * CAP:(f % 2 + 1) * CAP], ew1[:, e % 2, f * P:(f + 1) * P],
                                  dT[:, e % 2, :], start=True, stop=True)
                m.then_inc(m_h, 1)
                pe.wait_ge(m_hc, 2 * e + 2)
                if e >= 2:
                    pe.wait_ge(m_yc, e - 1)
                for c in range(2):
                    for f in range(4):
                        m = pe.matmul(bank[0:HC, 4 + e % 2, c * P:(c + 1) * P], eh[:, e % 2, f // 2, f % 2, c * HC:(c + 1) * HC],
                                      ew2[:, e % 2, f, :], start=(f == 0), stop=(f == 3))
                m.then_inc(m_y, 1)
            pe.wait_ge(m_yc, NE)
            xflat = xT[:, :, :].rearrange("p b t -> p (b t)")
            for q in range(4):
                for i in range(4 * q, 4 * q + 4):
                    t = pe.transpose(bank[:, (6, 7, 0, 1)[q], (i % 4) * P:(i % 4 + 1) * P], xflat[:, i * P:(i + 1) * P], ident[:, :])
                t.then_inc(m_xo, 1)

        @block.scalar
        def _(act):
            def attention(a):
                base = ATT1 if a else 0
                with act.Fori(0, BATCH) as b:
                    k, n = base + b, a * BATCH + b
                    act.wait_ge(step_done, k + 1)
                    ln_scalar(act, k, 1)
                    if a == 0:
                        act.wait_ge(a_lat, 2 * n + 1)
                        act.activation(cq, bank[0:64, 2, :], ACT.Identity, bias=bias[0:64, 0:1]).then_inc(a_latc, 1)
                        act.wait_ge(a_lat, 2 * n + 2)
                        act.activation(ckv, bank[0:64, 3, :], ACT.Identity, bias=bias[0:64, 1:2]).then_inc(a_latc, 1)
                    act.wait_ge(a_v, n + 1)
                    act.wait_ge(a_clr, 3 * a + 3)
                    act.activation(va[:, :, :, 0:AD], bank[:, 0, :].rearrange("p (c h d) -> p c h d", c=TILES, h=AH),
                                   ACT.Copy).then_inc(a_vc, 1)
                    for half in range(2):
                        act.wait_ge(a_sk, 2 * n + half + 1)
                        act.activation(kst[:, 4 * half:4 * half + 4, :], bank[:, 4 * half:4 * half + 4, :], ACT.Identity,
                                       bias=onesrow[:, 0:1]).then_inc(a_ke, 1)
                    act.wait_ge(m_zero, 5 * 16)
                    act.wait_ge(zeros_set, 2 * a + 1)
                    for half in range(2):
                        act.wait_ge(a_sq, 2 * n + half + 1)
                        act.activation(qst[0:64, 4 * half:4 * half + 4, 0, :], bank[0:64, 4 * half:4 * half + 4, :],
                                       ACT.Copy).then_inc(a_qe, 1)
                    act.wait_ge(a_t, n + 1)
                    act.activation(nmT, bank[:, 0, :], ACT.Copy).then_inc(a_tc, 1)
                    for half in range(2):
                        act.wait_ge(a_sm, 2 * n + half + 1)
                        act.activation(qst[MAX_ROW:MAX_ROW + 3, 4 * half:4 * half + 4, 0, :],
                                       bank[MAX_ROW:MAX_ROW + 3, 4 * half:4 * half + 4, :], ACT.Copy).then_inc(a_me, 1)
                    for i in range(PAIRQ):
                        act.wait_ge(a_st, n * PAIRQ + i + 1)
                        u, half = divmod(i, 2)
                        if u >= 2:
                            act.wait_ge(a_pv, n * UNITS + u - 1)
                        q = 2 * (i % 3)
                        act.activation(pT[:, u % 2, 2 * half:2 * half + 2, :], bank[:, q:q + 2, :], ACT.Exp).then_inc(a_p, 1)
                    act.wait_ge(a_ot, (n + 1) * TILES)
                    act.activation(oT, bank[:, 4, :], ACT.Identity,
                                   bias=bias[:, 8 + 6 * a:9 + 6 * a]).then_inc(a_otc, 1)

            for b in range(BATCH):
                act.wait_ge(x_tr, b + 1)
                act.activation(xT[:, b, :], bank[:, b, :], ACT.Copy).then_inc(x_in, 1)
            act.wait_ge(ld_c, LOADED)
            act.wait_ge(init, 5)
            attention(0)
            with act.Fori(0, BATCH) as b:
                act.wait_ge(step_done, SEED + b + 1)
                ln_scalar(act, SEED + b, 1)
            def tiles(l, b, tail):
                it = l * BATCH + b
                if tail:
                    act.wait_ge(l_v, 4 * TILES * it)
                    settle(act)
                act.activation(xs[0:64, WIN:], zT[0:64, b, :], ACT.Copy).then_inc(l_xs, 1)

                def squares(i):
                    T = it * TILES + i
                    act.wait_ge(l_qk, T + 1)
                    act.activation(sq, bank[:, 0:4, :].rearrange("p a t -> p (a t)"), ACT.Square).then_inc(l_sq, 1)

                def values(i):
                    T = it * TILES + i
                    for w in range(4):
                        act.wait_ge(l_v, 4 * T + w + 1)
                        for r in range(2):
                            act.activation(vD[64 * r:64 * r + 64, w, :, r, :],
                                           bank[64 * r:64 * r + 64, 6 + w % 2, :].rearrange("p (c d) -> p c d", d=LD),
                                           ACT.Copy).then_inc(l_vc, 1)

                squares(0)
                values(0)
                if tail:
                    shift_half(it - 1, b - 1)
                    ln_scalar(act, LAYER0 + it - 1, 4)
                squares(1)
                for i in range(TILES):
                    T = it * TILES + i
                    act.wait_ge(l_tr, 2 * T + 1)
                    act.activation(qT[:, i % 2, :, :], bank[:, 4:6, :].rearrange("p a (c t) -> p (a c) t", t=P), ACT.Copy).then_inc(l_trc, 1)
                    act.wait_ge(l_tr, 2 * T + 2)
                    settle(act)
                    for r in range(2):
                        act.activation(kD[64 * r:64 * r + 64, i % 2, :, r, WIN:],
                                       bank[64 * r:64 * r + 64, 6:8, :].rearrange("p a (c t) -> p (a c) t", t=P), ACT.Copy).then_inc(l_trc, 1)
                    if tail and i == 1:
                        gate(it - 1, 0)
                        gate(it - 1, 1)
                    if tail and i == 2:
                        gate(it - 1, 2)
                    act.wait_ge(l_e, T + 1)
                    act.activation(sc[:, 1, :], sc[:, 0, :], ACT.Exp, scale=8.0).then_inc(l_p, 1)
                    act.wait_ge(l_pt, T + 1)
                    act.activation(sc[:, 3, :], bank[:, 6:8, :].rearrange("p a t -> p (a t)"), ACT.Copy).then_inc(l_ptc, 1)
                    if i + 2 < TILES:
                        squares(i + 2)
                    if i + 1 < TILES:
                        act.wait_ge(l_pv, T + 1)
                        settle(act)
                        values(i + 1)
                    act.wait_ge(l_ot, T + 1)
                    act.activation(oTl[:, :, i * P:(i + 1) * P],
                                   bank[:, 6:8, :].rearrange("p a (c t) -> p (a c) t", t=P), ACT.Copy).then_inc(l_oc, 1)

            def shift_half(it, b):
                act.wait_ge(l_res, it + 1)
                settle(act)
                act.activation(xf[0:64, :], zT[0:64, b, :], ACT.Copy).then_inc(l_xf, 1)

            def gate(it, j):
                n = FCH[j][1]
                act.wait_ge(f_h, 6 * it + 2 * j + 1)
                act.activation(gates[0:n, j, :], bank[0:n, 2 * (j % 2), :], ACT.Gelu, bias=lb[0:n, 6 + j:7 + j]).then_inc(f_g, 1)

            with act.Fori(0, DEPTH) as l:
                act.wait_ge(zeros_set, 2)
                act.wait_ge(step_done, l * BATCH + LAYER0 + 1)
                settle(act)
                tiles(l, 0, False)
                act.wait_ge(ld_f, l * LDF + LDF)
                settle(act)
                with act.Fori(1, BATCH) as b:
                    tiles(l, b, True)
                last = l * BATCH + BATCH - 1
                shift_half(last, BATCH - 1)
                ln_scalar(act, LAYER0 + last, 4)
                for j in range(3):
                    gate(last, j)
            attention(1)
            with act.Fori(0, BATCH) as b:
                act.wait_ge(step_done, MOE0 + b + 1)
                ln_scalar(act, MOE0 + b, 1)
            act.wait_ge(m_tk, 1)
            for q in range(4):
                act.activation(xtok[:, 4 * q:4 * q + 4, :], bank[:, 3 + q, :].rearrange("p (a d) -> p a d", d=P), ACT.Copy).then_inc(m_tkc, 1)
            act.wait_ge(m_sh, 1)
            act.activation(rt[:, 1, :], rt[:, 0, :], ACT.Exp).then_inc(m_ex, 1)
            for e in range(NE):
                act.wait_ge(m_h, e + 1)
                if e >= 2:
                    act.wait_ge(m_y, e - 1)
                for r in range(2):
                    act.activation(eh[:, e % 2, r, :, :], bank[:, 2 + r, 0:2 * CAP].rearrange("p (c t) -> p c t", c=2),
                                   ACT.Gelu_apprx_tanh).then_inc(m_hc, 1)

        def out_rows(dve, e):
            dve.wait_ge(m_y, e + 1)
            if e >= 2:
                dve.wait_ge(m_yo[e % 2], 16 * (e // 2))
            dve.tensor_copy(yo[:, e % 2, :, :], bank[0:HC, 4 + e % 2, 0:2 * P].rearrange("p (c d) -> p c d", c=2)).then_inc(m_yc, 1)

        @block.vector
        def _(dve):
            NEWTON = 2 + 3 * 3

            def inverse_root(ch, out, s):
                u = small[:, 5, :]
                ch.link(dve.tensor_scalar(s, s, 1e-24, None, ALU.max))
                ch.link(dve.tensor_scalar(out.bitcast(I32), s.bitcast(I32), -0.5, float(0x5F3759DF), ALU.mult, ALU.add))
                for _ in range(3):
                    ch.link(dve.scalar_tensor_tensor(out=u, in0=s, scalar=-0.5, in1=out, op0=ALU.mult, op1=ALU.mult))
                    ch.link(dve.tensor_tensor(u, u, out, ALU.mult))
                    ch.link(dve.scalar_tensor_tensor(out=out, in0=u, scalar=1.5, in1=out, op0=ALU.add, op1=ALU.mult))


            def attention(a):
                base = ATT1 if a else 0
                with dve.Fori(0, BATCH) as b:
                    k, n = base + b, a * BATCH + b
                    dve.wait_ge(step_done, k + 1)
                    ln_vector(dve, k, xT[:, b, :], xn[:, :], 0, 1)
                    ch = Chain(dve, (a_ch, a_ch1)[a], b * (16 - 2 * a))
                    for which in range(2):
                        dve.wait_ge((a_q, a_k)[which], n + 1)
                        plain, swap, up = ((5, 6, 4), (2, 3, 7))[which]
                        c = (4 + 6 * a) + 2 * which
                        dst = (qf, kf)[which]
                        ch.link(dve.scalar_tensor_tensor(out=tA, in0=bank[:, plain, :], scalar=bias[:, c:c + 1],
                                                         in1=ropeC[:, a, :], op0=ALU.add, op1=ALU.mult))
                        ch.link(dve.scalar_tensor_tensor(out=tB, in0=bank[:, swap, :], scalar=bias[:, c + 1:c + 2],
                                                         in1=ropeS[:, a, :], op0=ALU.add, op1=ALU.mult))
                        if a == 0:
                            ch.link(dve.tensor_tensor(tA, tA, tB, ALU.add))
                            ch.link(dve.scalar_tensor_tensor(out=dst, in0=bank[:, up, :], scalar=bias[:, 2 + which:3 + which],
                                                             in1=tA, op0=ALU.add, op1=ALU.add))
                        else:
                            ch.link(dve.tensor_tensor(dst, tA, tB, ALU.add))
                        if which == 0:
                            ch.link(dve.tensor_scalar(dst, dst, 1.0 / SCALE[a], None, ALU.mult))
                        high, middle, low = (parts[:, 3 * which + p, :] for p in range(3))
                        done = (a_qf, a_kf)[which]
                        dve.tensor_copy(high, dst).then_inc(done, 1)
                        dve.wait_ge(done, 3 * n + 1)
                        ch.link(dve.tensor_tensor(tC, dst, high, ALU.subtract))
                        dve.tensor_copy(middle, tC).then_inc(done, 1)
                        dve.wait_ge(done, 3 * n + 2)
                        dve.tensor_tensor(low, tC, middle, ALU.subtract).then_inc(done, 1)
                    dve.wait_ge(m_zero, 5 * 16)
                    dve.wait_ge(zeros_set, 2 * a + 1)
                    for half in range(2):
                        dve.wait_ge(a_sq, 2 * n + half + 1)
                        dve.tensor_copy(qst[64:P, 4 * half:4 * half + 4, 1, :], bank[64:P, 4 * half:4 * half + 4, :]).then_inc(a_qo, 1)
                    dve.wait_ge(a_clr, 3 * a + 3)
                    for u in range(UNITS):
                        qt, j = divmod(u, HG)
                        dve.wait_ge(a_s, n * UNITS + u + 1)
                        dve.tensor_reduce(nm[:, qt, HG * j:HG * j + HG], bank[:, 4 * (u % 2):4 * (u % 2) + 4, :], AX.X, ALU.max,
                                          negate=True).then_inc(a_mx, 1)
                    dve.wait_ge(a_mx, (n + 1) * UNITS)
                    ch.link(dve.tensor_copy(nmb, nm))
                    ch.link(dve.tensor_copy(nmp[:, :, 0:AH], nmb))
                    ch.link(dve.tensor_tensor(nmr, nm, nmb, ALU.subtract))
                    ch.link(dve.tensor_copy(nmb, nmr))
                    ch.link(dve.tensor_copy(nmp[:, :, 32:32 + AH], nmb))
                    dve.tensor_tensor(nmp[:, :, 64:64 + AH], nmr, nmb, ALU.subtract).then_inc(a_nm, 1)
                    for half in range(2):
                        dve.wait_ge(a_sm, 2 * n + half + 1)
                        dve.tensor_copy(qst[64 + MAX_ROW:64 + MAX_ROW + 3, 4 * half:4 * half + 4, 1, :],
                                        bank[64 + MAX_ROW:64 + MAX_ROW + 3, 4 * half:4 * half + 4, :]).then_inc(a_mo, 1)
                    for j in range(HG):
                        dve.wait_ge(a_pv, n * UNITS + (j + 1) * TILES)
                        dve.tensor_copy(oU[:, j, :], bank[:, 6 + j % 2, :]).then_inc(a_oc, 1)
                    for qt in range(TILES):
                        dve.wait_ge(a_ob, n * TILES + qt + 1)
                        o4 = bank[:, qt, :].rearrange("p (j g e) -> p j g e", j=HG, g=4)
                        r3 = rinv[:, qt * AH:(qt + 1) * AH].rearrange("p (j g) -> p j g", j=HG)
                        dve.reciprocal(r3, o4[:, :, :, AD]).then_inc(a_rc, 1)
                        dve.wait_ge(a_rc, n * TILES + qt + 1)
                        if qt >= 2:
                            dve.wait_ge(a_ot, n * TILES + qt - 1)
                        dve.tensor_tensor(on[:, qt % 2, :].rearrange("p (j g d) -> p j g d", g=4, d=AD), o4[:, :, :, 0:AD],
                                          r3.unsqueeze(3).broadcast_to([P, HG, 4, AD]), ALU.mult).then_inc(a_on, 1)
                    dve.wait_ge(a_wo, n + 1)
                    dve.scalar_tensor_tensor(out=xT[:, b, :], in0=bank[:, 5, :], scalar=bias[:, 9 + 6 * a:10 + 6 * a],
                                             in1=xT[:, b, :], op0=ALU.add, op1=ALU.add).then_inc(step_done, 1)

            dve.wait_ge(ld_c, LOADED)
            dve.wait_ge(x_in, BATCH)
            dve.tensor_copy(maskw[:, :, :].rearrange("p a t -> p (a t)"), mask_f[:, 0:256]).then_inc(masks_set, 1)
            dve.tensor_copy(maskr[:, :], mask_f[:, 256:768]).then_inc(masks_set, 1)
            dve.wait_ge(init, 5)
            dve.wait_ge(masks_set, 2)
            dve.memset(tick[:, :], 0.0).then_inc(step_done, 1)
            attention(0)
            with dve.Fori(0, BATCH) as b:
                k = SEED + b
                dve.wait_ge(step_done, k + 1)
                ln_vector(dve, k, xT[:, b, :], zT[:, b, :], 0, 1)
                dve.wait_ge(ln_out, k + 1)
                dve.memset(tick[:, :], 0.0).then_inc(step_done, 1)
            ss, nrm = small[:, 0, :], small[:, 1, :]
            mx, den, rden = small[:, 2, 0:LH], small[:, 3, 0:LH], small[:, 4, 0:LH]

            def tiles(l, b, tail):
                it = l * BATCH + b
                if tail:
                    dve.wait_ge(l_v, 4 * TILES * it)
                    settle(dve)
                dve.tensor_copy(xs[64:P, WIN + 1:], zT[64:P, b, 0:SEQ - 1]).then_inc(l_xs, 1)

                def norm(i):
                    T = it * TILES + i
                    ch = Chain(dve, l_chr, T * (NEWTON + 1))
                    dve.wait_ge(l_sq, T + 1)
                    ch.link(dve.tensor_reduce(ss, sq.rearrange("p (h d) -> p h d", d=LD), AX.X, ALU.add))
                    inverse_root(ch, nrm, ss)
                    dve.tensor_tensor(qn.rearrange("p (h d) -> p h d", d=LD),
                                      bank[:, 0:4, :].rearrange("p a (h d) -> p (a h) d", d=LD),
                                      nrm.unsqueeze(2).broadcast_to([P, 2 * LH, LD]), ALU.mult).then_inc(l_qn, 1)

                def rotate_1(i):
                    T = it * TILES + i
                    dve.wait_ge(l_qn, T + 1)
                    if i >= 1 or tail:
                        dve.wait_ge(l_yk, T)
                    dve.tensor_tensor(rotA.rearrange("p (a h d) -> p a h d", a=2, h=LH), qn.rearrange("p (a h d) -> p a h d", a=2, h=LH),
                                      rotCl[:, i, :].rearrange("p (a d) -> p a d", a=2).unsqueeze(2).broadcast_to([P, 2, LH, LD]),
                                      ALU.mult).then_inc(l_ra, 1)

                def rotate_2(i):
                    T = it * TILES + i
                    dve.wait_ge(l_ra, T + 1)
                    dve.wait_ge(l_rb, 2 * T + 2)
                    dve.tensor_tensor(rotB[:, 0:INNER], rotA[:, 0:INNER], rotB[:, 0:INNER], ALU.add).then_inc(l_yq, 1)

                def softmax(i):
                    T = it * TILES + i
                    ch = Chain(dve, l_chs, T * 3)
                    dve.wait_ge(l_s, T + 1)
                    s3 = bank[:, 4:6, :].rearrange("p a (h j) -> p (a h) j", j=64)
                    ch.link(dve.tensor_reduce(mx, s3, AX.X, ALU.max))
                    dve.tensor_tensor(sc[:, 0, :].rearrange("p (h j) -> p h j", j=64), s3,
                                      mx.unsqueeze(2).broadcast_to([P, LH, 64]), ALU.subtract).then_inc(l_e, 1)

                def sums(i):
                    T = it * TILES + i
                    ch = Chain(dve, l_chs, T * 3 + 1)
                    dve.wait_ge(l_p, T + 1)
                    ch.link(dve.tensor_reduce(den, sc[:, 1, :].rearrange("p (h j) -> p h j", j=64), AX.X, ALU.add))
                    ch.link(dve.reciprocal(rden, den))

                def normalise(i):
                    T = it * TILES + i
                    dve.wait_ge(l_pv, T + 1)
                    dve.tensor_tensor(sc[:, 2, :].rearrange("p (h d) -> p h d", d=LD),
                                      bank[:, 4:6, :].rearrange("p a (h d) -> p (a h) d", d=LD),
                                      rden.unsqueeze(2).broadcast_to([P, LH, LD]), ALU.mult).then_inc(l_on, 1)

                def rotate(i):
                    norm(i)
                    if i == 0 and tail:
                        residual(it - 1, b - 1)
                    rotate_1(i)

                rotate(0)
                if tail:
                    centre(it - 1)
                rotate_2(0)
                rotate(1)
                for i in range(TILES):
                    if tail and i == 1:
                        hidden(it - 1, 0)
                        hidden(it - 1, 1)
                    if tail and i == 2:
                        hidden(it - 1, 2)
                    softmax(i)
                    if tail and i == 0:
                        scale_norm(it - 1)
                    if tail and i == 3:
                        ffn_end(it - 1, b - 1)
                    sums(i)
                    if i + 1 < TILES:
                        rotate_2(i + 1)
                    normalise(i)
                    if i + 2 < TILES:
                        rotate(i + 2)

            def residual(it, b):
                dve.wait_ge(l_wo, it + 1)
                dve.tensor_tensor(zT[:, b, :], bank[:, 4, :], zT[:, b, :], ALU.add).then_inc(l_res, 1)
                dve.wait_ge(l_res, it + 1)
                settle(dve)
                dve.tensor_copy(xf[64:P, 1:], zT[64:P, b, 0:SEQ - 1]).then_inc(l_xf, 1)

            def centre(it):
                dve.wait_ge(l_xf, 2 * it + 2)
                ln_centre(dve, LAYER0 + it, xf[:, :], 5)

            def scale_norm(it):
                ln_scale(dve, LAYER0 + it, sqn[:, :])
                dve.wait_ge(ln_out, LAYER0 + it + 1)
                dve.tensor_scalar(xn[:, :], sqn[:, :], lb[:, 0:1], lb[:, 1:2], ALU.mult, ALU.add).then_inc(l_fn, 1)

            def hidden(it, j):
                n = FCH[j][1]
                dve.wait_ge(f_h, 6 * it + 2 * j + 2)
                dve.wait_ge(f_g, 3 * it + j + 1)
                dve.scalar_tensor_tensor(out=hT[0:n, j, :], in0=bank[0:n, 2 * (j % 2) + 1, :], scalar=lb[0:n, 3 + j:4 + j],
                                         in1=gates[0:n, j, :], op0=ALU.add, op1=ALU.mult).then_inc(f_hd, 1)

            def ffn_end(it, b):
                dve.wait_ge(f_y, it + 1)
                dve.scalar_tensor_tensor(out=zT[:, b, :], in0=bank[:, 2, :], scalar=lb[:, 2:3],
                                         in1=zT[:, b, :], op0=ALU.add, op1=ALU.add).then_inc(step_done, 1)

            with dve.Fori(0, DEPTH) as l:
                dve.wait_ge(ld_qkv, l * LDQ + LDQ)
                dve.wait_ge(step_done, l * BATCH + LAYER0 + 1)
                h = LD // 2
                qk2 = qks[:, :, :]
                dve.tensor_tensor(rotCl[:, :, :].rearrange("p c (a d) -> p c a d", a=2), rotC[:, :, :].rearrange("p c (a d) -> p c a d", a=2),
                                  qk2.unsqueeze(1).broadcast_to([P, TILES, 2, LD]), ALU.mult).then_inc(l_tab, 1)
                for lo in range(2):
                    o, s = (slice(0, h), slice(h, LD)) if lo == 0 else (slice(h, LD), slice(0, h))
                    dve.tensor_tensor(rotSl[:, :, :].rearrange("p c (a d) -> p c a d", a=2)[:, :, :, o],
                                      rotS[:, :, :].rearrange("p c (a d) -> p c a d", a=2)[:, :, :, o],
                                      qk2[:, :, s].unsqueeze(1).broadcast_to([P, TILES, 2, h]), ALU.mult).then_inc(l_tab, 1)
                dve.wait_ge(l_tab, l * 3 + 3)
                settle(dve)
                tiles(l, 0, False)
                dve.wait_ge(ld_f, l * LDF + LDF)
                settle(dve)
                with dve.Fori(1, BATCH) as b:
                    tiles(l, b, True)
                last = l * BATCH + BATCH - 1
                residual(last, BATCH - 1)
                centre(last)
                scale_norm(last)
                for j in range(3):
                    hidden(last, j)
                ffn_end(last, BATCH - 1)
            with dve.Fori(0, BATCH) as b:
                dve.wait_ge(step_done, ATT1 + 1)
                dve.tensor_tensor(xT[:, b, :], xT[:, b, :], zT[:, b, :], ALU.add).then_inc(x_sum, 1)
            dve.wait_ge(x_sum, BATCH)
            attention(1)
            with dve.Fori(0, BATCH) as b:
                k = MOE0 + b
                dve.wait_ge(step_done, k + 1)
                ln_vector(dve, k, xT[:, b, :], zT[:, b, :], 0, 1)
                dve.wait_ge(ln_out, k + 1)
                dve.memset(tick[:, :], 0.0).then_inc(step_done, 1)
            def g3(j):
                return rt[:, j, :].rearrange("p (i e) -> p i e", e=NE)

            def bc(v):
                return v.unsqueeze(2).broadcast_to([P, NT, NE])

            def per_e(j):
                return moe_c[:, j, :].unsqueeze(1).broadcast_to([P, NT, NE])

            mxl, mxv, sume, prob, s1, r1, keep, wgt = (rs[:, j, 0:NT] for j in range(8))
            ch = Chain(dve, m_ch, 0)
            dve.wait_ge(m_lg, 1)
            lg = bank[:, 2, 0:256].rearrange("p (i e) -> p i e", e=NE)
            ch.link(dve.tensor_reduce(mxl, lg, AX.X, ALU.max))
            dve.tensor_tensor(g3(0), lg, bc(mxl), ALU.subtract).then_inc(m_sh, 1)
            dve.wait_ge(m_sh, 1)
            ch.link(dve.scalar_tensor_tensor(out=g3(2), in0=g3(0), scalar=0.0, in1=per_e(0), op0=ALU.is_equal, op1=ALU.mult))
            ch.link(dve.tensor_reduce(mxv, g3(2), AX.X, ALU.max))
            dve.tensor_tensor(g3(3), g3(2), bc(mxv), ALU.is_equal).then_inc(m_oh, 1)
            dve.wait_ge(m_ex, 1)
            ch.link(dve.tensor_reduce(sume, g3(1), AX.X, ALU.add))
            ch.link(dve.reciprocal(prob, sume))
            ch.link(dve.memset(rt[:, 4, 0:NE], 0.0))
            dve.wait_ge(m_cum, 1)
            for i in range(1, NT):
                ch.link(dve.tensor_tensor(rt[:, 4, i * NE:(i + 1) * NE], rt[:, 4, (i - 1) * NE:i * NE],
                                          bank[:, 0, (i - 1) * NE:i * NE], ALU.add))
            ch.link(dve.tensor_tensor(rt[:, 5, :], rt[:, 4, :], bank[:, 7, 0:256], ALU.add))
            ch.link(dve.tensor_tensor(rt[:, 6, :], rt[:, 5, :], rt[:, 3, :], ALU.mult))
            ch.link(dve.tensor_reduce(r1, g3(6), AX.X, ALU.add))
            ch.link(dve.tensor_tensor(g3(7), g3(5), per_e(1), ALU.add))
            ch.link(dve.tensor_tensor(rt[:, 2, :], rt[:, 7, :], rt[:, 3, :], ALU.mult))
            ch.link(dve.tensor_reduce(s1, g3(2), AX.X, ALU.add))
            ch.link(dve.tensor_scalar(keep, r1, float(CAP), None, ALU.is_le))
            ch.link(dve.tensor_tensor(wgt, keep, prob, ALU.mult))
            ch.link(dve.tensor_tensor(r1, s1, moe_c[:, 2, :], ALU.subtract))
            ch.link(dve.tensor_tensor(r1, r1, keep, ALU.mult))
            ch.link(dve.tensor_tensor(r1, r1, moe_c[:, 2, :], ALU.add))
            dve.tensor_copy(idx[:, 0, :], r1).then_inc(m_idx, 1)
            ch.link(dve.tensor_tensor(s1, s1, keep, ALU.mult))
            dve.tensor_copy(idx[:, 1, :], s1).then_inc(m_idx, 1)
            for e in range(NE):
                dve.wait_ge(m_d, e + 1)
                if e >= 2:
                    dve.wait_ge(m_h, e - 1)
                dve.tensor_copy(dT[:, e % 2, :], bank[:, e % 2, 0:CAP]).then_inc(m_dc, 1)
                if e >= 1:
                    out_rows(dve, e - 1)
            out_rows(dve, NE - 1)
            for q in range(4):
                dve.wait_ge(m_xo, q + 1)
                dve.wait_ge(m_g, 16 * NT)
                for i in range(4 * q, 4 * q + 4):
                    last = dve.scalar_tensor_tensor(out=fin[:, i, :], in0=gat[:, i, :], scalar=wgt[:, i:i + 1],
                                                    in1=bank[:, (6, 7, 0, 1)[q], (i % 4) * P:(i % 4 + 1) * P],
                                                    op0=ALU.mult, op1=ALU.add)
                last.then_inc(m_fin, 1)


def constants():
    f = np.float32
    c = {"c_ident": np.eye(P, dtype=f), "c_mean": np.full((P, P), 1.0 / P, f)}
    c["c_upper"] = np.triu(np.ones((P, P), f))
    pos = np.arange(SEQ, dtype=f)
    ids = np.arange(P // 2, dtype=f)
    theta0 = (f(10000.0) ** (f(-2.0) * ids) / f(P // 2)).astype(f)
    ang0 = (pos[:, None] * theta0[None, :]).astype(f)
    theta1 = (f(10000.0) ** (f(-2.0) * np.arange(AD // 2, dtype=f) / f(AD))).astype(f)
    ang1 = (pos[:, None] * theta1[None, :]).astype(f)
    j = np.arange(P)
    a0, a1 = ang0[:, j // 2].T.astype(np.float64), ang1[:, (j % AD) // 2].T.astype(np.float64)
    s0 = np.where(j % 2 == 0, -1.0, 1.0)[:, None]
    s1 = np.where(j % AD < AD // 2, -1.0, 1.0)[:, None]
    c["c_ropeC"] = np.stack([np.cos(a0), np.cos(a1)], 1).astype(f)
    c["c_ropeS"] = np.stack([np.sin(a0) * s0, np.sin(a1) * s1], 1).astype(f)
    one = np.uint16(0x3F80)
    selq, selk = (np.zeros((P, 3, AH, 64), np.uint16) for _ in range(2))
    selm = np.zeros((P, AH, 32), np.uint16)
    c["c_onesrow"] = np.zeros((P, 1), f)
    for h in range(AH):
        for (pq, pk), row in zip(STACK, STACK_ROW):
            for d in range(AD):
                selq[AD * h + d, pq, h, row + d] = one
                selk[AD * h + d, pk, h, row + d] = one
        for part in range(3):
            selm[32 * part + h, h, part] = one
    for r in range(2):
        c["c_onesrow"][64 * r + MAX_ROW:64 * r + MAX_ROW + 3] = 1.0
    c["c_selq"], c["c_selk"] = (v.reshape(P, 3, 1024).view(f) for v in (selq, selk))
    c["c_selm"] = selm.reshape(P, 512).view(f)
    half = np.arange(0, LD, 2, dtype=f)
    inv_freq = (f(1.0) / f(10000.0) ** (half / f(LD))).astype(f)
    fr = (pos[:, None] * inv_freq[None, :]).astype(f).astype(np.float64)
    base = ((half + f(0.4 * LD)) / f(1.4 * LD)).astype(f)
    power = ((pos - SEQ // 2) / f(WIN // 2)).astype(f)
    scale = (base[None, :].astype(np.float64) ** power[:, None].astype(np.float64)).astype(f).astype(np.float64)
    tabs = []
    for t, sign in ((np.cos(fr), (1, 1)), (np.sin(fr), (-1, 1))):
        full = []
        for s in (scale, 1.0 / scale):
            full.append(np.concatenate([sign[0] * t * s, sign[1] * t * s], 1))
        tabs.append(np.concatenate(full, 1).reshape(TILES, P, 2 * LD).transpose(1, 0, 2).astype(f))
    c["c_rotC"], c["c_rotS"] = tabs
    w = np.zeros((P, 2, P), f)
    w[np.arange(P) % WIN, :, np.arange(P)] = 1.0
    w[WIN, 0, 0:WIN] = 1.0
    ii, jj = np.arange(WIN)[:, None], np.arange(2 * WIN)[None, :]
    m = np.zeros((P, 2 * WIN), f)
    m[0:WIN] = np.where((jj < ii) | (jj > ii + WIN), f(NEG), f(0.0))
    m[WIN, 0:WIN] = NEG
    c["c_maskw"] = w.reshape(P, 2 * P)
    c["c_maskr"] = np.tile(m, (1, PAIRS)).astype(f)
    e = np.arange(NE, dtype=f)
    moe = np.zeros((P, 3, NE), f)
    moe[:, 0, :] = NE - e
    moe[:, 1, :] = e * CAP - 1
    moe[:, 2, :] = SLOTS + np.arange(NT)[None, :] * P + np.arange(P)[:, None]
    c["c_moe"] = moe
    return c


def kernel(**inputs):
    import concourse.bacc as _bacc
    from concourse.bass_utils import run_bass_kernel_spmd as _run

    swap0 = np.arange(P) ^ 1
    swap1 = (np.arange(P) // AD) * AD + (np.arange(P) % AD + AD // 2) % AD
    a = {n: np.ascontiguousarray(v) for n, v in inputs.items()}
    a.update(constants())
    a["wqr_swapped"] = np.ascontiguousarray(a["L0_attn_Wq_r_w"][:, swap0])
    a["wkr_swapped"] = np.ascontiguousarray(a["L0_attn_Wk_r_w"][:, swap0])
    a["bqr_swapped"] = np.ascontiguousarray(a["L0_attn_Wq_r_b"][swap0])
    a["bkr_swapped"] = np.ascontiguousarray(a["L0_attn_Wk_r_b"][swap0])
    for n in "qkvo":
        a[f"w{n}_t"] = np.ascontiguousarray(a.pop(f"L1_attn_w{n}").T)
    for n in "qk":
        a[f"w{n}_swapped"] = np.ascontiguousarray(a[f"w{n}_t"][:, swap1])
        a[f"b{n}_swapped"] = np.ascontiguousarray(a[f"L1_attn_b{n}"][swap1])
    a["gate_t"] = np.ascontiguousarray(a.pop("L1_ffn_gate_w").T)
    nc = _bacc.Bacc("TRN2", target_bir_lowering=False, num_devices=1)
    arrays, aps = {}, {}
    for name, v in a.items():
        arrays[f"in_{name}"] = v
        aps[name] = nc.dram_tensor(f"in_{name}", v.shape, mybir.dt.from_np(v.dtype), kind="ExternalInput").ap()
    out = nc.dram_tensor("out_0", (BATCH, SEQ, P), F32, kind="ExternalOutput").ap()
    build(nc, aps, out)
    r = _run(nc, [arrays], core_ids=[0])
    return r.results[0]["out_0"]
```

```python
from contextlib import ExitStack

import concourse.bass as bass
from concourse import mybir
import numpy as np

F32 = mybir.dt.float32
BF16 = mybir.dt.bfloat16
U32 = mybir.dt.uint32
I32 = mybir.dt.int32
ALU = mybir.AluOpType
ACT = mybir.ActivationFunctionType
AX = mybir.AxisListType

P = 128
BATCH, SEQ = 4, 512
TILES = SEQ // P
TOKENS = BATCH * SEQ
NT = TOKENS // P
EPS = 1e-5
AH, AD = 16, 8
HG = 4
PAIRS_A = AH // 2
UNITS = TILES * HG
PAIRQ = 2 * UNITS
STACK = [(0, 0), (0, 1), (1, 0), (1, 1), (0, 2), (2, 0)]
STACK_ROW = [0, 8, 16, 24, 40, 48]
MAX_ROW = 32
SROWS = 56
MUNITS = TILES * PAIRS_A
LEAD = [[1, 6, 14, 15, 17, 19, 21, 23, 25, 27, 29], [1, 6, 14, 16, 18, 20, 22]]
AV = 32
DEPTH, LH, LD, WIN = 6, 16, 64, 32
PAIRS = LH // 2
INNER = LH * LD
FF = int(P * 4 * 2 / 3)
FCH = [(0, 128), (128, 128), (256, FF - 256)]
NEG = -1e30
SCALE = [float(np.sqrt(np.float32(AH + 64 + 64))), float(np.sqrt(np.float32(AD)))]
PACKED = ["L0_attn_Wd_q_w+L0_attn_Wd_kv_w", "L0_attn_Wk_r_w", "wkr_swapped", "L0_attn_Wo_w", "wo_t",
          "wq_t", "wq_swapped", "wk_t", "wk_swapped", "wv_t"]
PACKED_LOW = ["L0_attn_Wu_q_w", "L0_attn_Wu_k_w", "L0_attn_Wu_v_w", "L0_attn_Wq_r_w", "wqr_swapped"]
BIASES = ["L0_attn_Wd_q_b", "L0_attn_Wd_kv_b", "L0_attn_Wu_q_b", "L0_attn_Wu_k_b",
          "L0_attn_Wq_r_b", "bqr_swapped", "L0_attn_Wk_r_b", "bkr_swapped", "L0_attn_Wu_v_b", "L0_attn_Wo_b",
          "L1_attn_bq", "bq_swapped", "L1_attn_bk", "bk_swapped", "L1_attn_bv", "L1_attn_bo"]
NE = 16
CAP = 160
HC = CAP // 2
SLOTS = NE * CAP


class Chain:

    def __init__(self, eng, sem, start):
        self.eng, self.sem, self.value = eng, sem, start

    def link(self, ins):
        ins.then_inc(self.sem, 1)
        self.value = self.value + 1
        self.eng.wait_ge(self.sem, self.value)


def build(nc, I, out):
    with ExitStack() as ctx:
        def sb(name, shape, dt=F32):
            return ctx.enter_context(nc.sbuf_tensor(name, shape, dt))

        def sem(name):
            return ctx.enter_context(nc.semaphore(name))

        bank = ctx.enter_context(nc.psum_tensor("bank", [P, 8, 512], F32))

        xT = sb("xT", [P, BATCH, SEQ])
        zT = sb("zT", [P, BATCH, SEQ])
        ident = sb("ident", [P, P])
        mean_w = sb("mean_w", [P, P])
        upper = sb("upper", [P, P])
        ropeC = sb("ropeC", [P, 2, SEQ])
        ropeS = sb("ropeS", [P, 2, SEQ])
        packed_m = sb("packed_m", [P, 256])
        sel_m = packed_m[:, :].bitcast(BF16)
        rotC = sb("rotC", [P, TILES, 2 * LD])
        rotS = sb("rotS", [P, TILES, 2 * LD])
        maskw = sb("maskw", [P, 2, P], BF16)
        maskr = sb("maskr", [P, 512], BF16)
        moe_c = sb("moe_c", [P, 3, NE])
        packed = sb("packed", [P, len(PACKED) * P])
        packed_low = sb("packed_low", [64, len(PACKED_LOW) * P])

        def pair(names, j, n=2):
            return names[:, j * P:(j + n) * P].rearrange("p (a d) -> p a d", d=P)

        wdq, wdkv = packed[:, 0:64], packed[:, 64:P]
        wkr, wo, wq1, wk1 = (pair(packed, j) for j in (1, 3, 5, 7))
        wv1 = packed[:, 9 * P:10 * P]
        wuq, wuk, wuv = (packed_low[:, j * P:(j + 1) * P] for j in range(3))
        wqr = pair(packed_low, 3)
        bias = sb("bias", [P, 16])
        wqkv = sb("wqkv", [P, 3 * INNER])
        wol = sb("wol", [P, PAIRS, P])
        w1 = sb("w1", [P, 2 * FF])
        w2 = sb("w2", [P, 3, P])
        lb = sb("lb", [P, 10])
        qks = sb("qks", [P, 2, LD])
        rotCl = sb("rotCl", [P, TILES, 2 * LD])
        rotSl = sb("rotSl", [P, TILES, 2 * LD])
        xc = sb("xc", [P, SEQ])
        sqn = sb("sqn", [P, SEQ])
        xn = xc
        tick = sb("tick", [P, 1])
        eps = sb("eps", [P, 1])
        xs = sb("xs", [P, 2, WIN + SEQ])
        kD = sb("kD", [P, 2, PAIRS, 2, WIN + P])
        qT = sb("qT", [P, 2, PAIRS, P])
        vbuf = sb("vbuf", [P, 4096])
        vD = vbuf[:, :].rearrange("p (w c r d) -> p w c r d", w=4, c=PAIRS, r=2)
        v2 = vbuf[:, :].rearrange("p (b w t) -> p b w t", b=2, w=4)
        big = sb("big", [P, 4, 2048])
        rotA, qn, sq, rotB = (big[:, j, :] for j in range(4))
        sc = sb("sc", [P, 4, 1024])
        mask_f = sc[:, 0, 0:768]
        oTl = sb("oTl", [P, PAIRS, SEQ])
        small = sb("small", [P, 8, 32])
        gates = sb("gates", [P, 3, SEQ])
        rstd = gates[:, 2, :]
        xf = gates[:, 0, :]
        hT = sb("hT", [P, 3, SEQ])
        cq, ckv = hT[0:64, 0, :], hT[0:64, 1, :]
        tA, tB = gates[:, 0, :], gates[:, 1, :]
        qf, kf = gates[:, 2, :], hT[:, 2, :]
        parts = big[:, 0, :].bitcast(BF16).rearrange("p (a t) -> p a t", t=SEQ)
        nmp = big[:, 1, 0:512].rearrange("p (q c) -> p q c", c=P)
        nm, nmr = (big[:, 1, c:c + 64].rearrange("p (q h) -> p q h", h=AH) for c in (512, 576))
        nmb = big[:, 1, 640:672].bitcast(BF16).rearrange("p (q h) -> p q h", h=AH)
        nmT = big[:, 1, 768:1024].bitcast(BF16)
        tC = big[:, 1, 1024:1536]
        pT = big[:, 2:4, :].rearrange("p b (g t) -> p b g t", g=HG)
        qst2 = oTl[:, :, :].rearrange("p a t -> p (a t)").bitcast(BF16).rearrange("p (r c) -> p r c", r=2)
        kst2 = vbuf[:, 0:2048].bitcast(BF16)
        qst = qst2.rearrange("p r (a t) -> p a r t", t=SEQ)
        kst = vbuf[:, 0:2048].bitcast(BF16).rearrange("p (a t) -> p a t", t=SEQ)
        va = v2[:, 1, :, :].rearrange("p c (h e) -> p c h e", h=AH)
        oU = sc[:, 0:2, :].rearrange("p a (b t) -> p (a b) t", b=2)
        rinv = small[:, 0:2, :].rearrange("p a b -> p (a b)")
        on = sc[:, 3, 0:256].rearrange("p (b t) -> p b t", b=2)
        oT = sc[:, 3, 512:1024]
        ones = rotCl[:, 0, :]
        xtok = sc[:, 0:2, :].rearrange("p a (b d) -> p (a b) d", d=P)
        idx = sb("idx", [P, 2, NT], U32)
        rt = big[:, 1:3, :].rearrange("p a (b t) -> p (a b) t", t=256)
        rs = small
        ew1 = wqkv[:, 0:1024].rearrange("p (b f) -> p b f", b=2)
        ew2 = wqkv[:, 1024:2048].rearrange("p (b f d) -> p b f d", b=2, f=4)
        xd = oTl[0:HC, :, :].rearrange("p a (b d) -> p (a b) d", d=P)
        dT = v2[:, 0, 0:2, 0:CAP]
        eh = v2[:, 1, :, 0:2 * CAP].rearrange("p (a b) (c t) -> p a b c t", a=2, c=2)
        yo = big[0:HC, 0, 0:512].rearrange("p (a c d) -> p a c d", a=2, c=2)
        gat = qT[:, :, :, :].rearrange("p a b d -> p (a b) d")
        fin = big[:, 3, :].rearrange("p (a d) -> p a d", d=P)

        disp = nc.dram_tensor("dispatch_rows", (SLOTS + TOKENS, P), F32, kind="Internal").ap()
        part_rows = nc.dram_tensor("part_rows", (2, SROWS // AD, 2, AD, AH // 2 * SEQ), BF16, kind="Internal").ap()
        yrow = nc.dram_tensor("expert_rows", (SLOTS, P), F32, kind="Internal").ap()

        kflat = kD[:, :, :, :, :].rearrange("p b c r t -> p (b c r t)")
        raw = kflat[:, 0:6 * SEQ].rearrange("p (a t) -> p a t", t=SEQ)
        vraw = kflat[:, 6 * SEQ:7 * SEQ]

        def projections(a):
            if a == 0:
                return [(wdq[:, :], xn[:, :], cq, bias[0:64, 0:1]), (wdkv[:, :], xn[:, :], ckv, bias[0:64, 1:2]),
                        (wqr[:, 0, :], cq, raw[:, 0, :], bias[:, 4:5]), (wqr[:, 1, :], cq, raw[:, 1, :], bias[:, 5:6]),
                        (wuq[:, :], cq, raw[:, 2, :], bias[:, 2:3]),
                        (wkr[:, 0, :], xn[:, :], raw[:, 3, :], bias[:, 6:7]), (wkr[:, 1, :], xn[:, :], raw[:, 4, :], bias[:, 7:8]),
                        (wuk[:, :], ckv, raw[:, 5, :], bias[:, 3:4])]
            return [(wq1[:, 0, :], xn[:, :], raw[:, 0, :], bias[:, 10:11]), (wq1[:, 1, :], xn[:, :], raw[:, 1, :], bias[:, 11:12]),
                    (wk1[:, 0, :], xn[:, :], raw[:, 3, :], bias[:, 12:13]), (wk1[:, 1, :], xn[:, :], raw[:, 4, :], bias[:, 13:14])]

        max_rows = I["c_maxrows"].bitcast(BF16)

        ld_x, ld_c = sem("ld_x"), sem("ld_c")
        init, zeros_set, settled, masks_set = sem("init"), sem("zeros_set"), sem("settled"), sem("masks_set")
        x_tr, x_in = sem("x_tr"), sem("x_in")
        ln_mean, ln_c, ln_sq, ln_var, ln_r, ln_i, ln_out = (
            sem(n) for n in ("ln_mean", "ln_c", "ln_sq", "ln_var", "ln_r", "ln_i", "ln_out"))
        step_done = sem("step_done")
        a_vc = sem("a_vc")
        a_qf, a_kf, a_ch, a_ch1, a_chm, a_rc = sem("a_qf"), sem("a_kf"), sem("a_ch"), sem("a_ch1"), sem("a_chm"), sem("a_rc")
        a_nm, a_tc, a_sm, a_me, a_mo, a_one, a_scr, a_stk = (
            sem(n) for n in ("a_nm", "a_tc", "a_sm", "a_me", "a_mo", "a_one", "a_scr", "a_stk"))
        a_last = sem("a_last")
        x_sum = sem("x_sum")
        a_prj, a_raw = [[sem(f"{n}{j}") for j in range(2)] for n in ("a_prj", "a_raw")]
        a_clr, a_s, a_mx, a_t, a_st, a_p, a_pv, a_oc, a_ob = (
            sem(n) for n in ("a_clr", "a_s", "a_mx", "a_t", "a_st", "a_p", "a_pv", "a_oc", "a_ob"))
        a_on, a_ot, a_otc, a_wo = sem("a_on"), sem("a_ot"), sem("a_otc"), sem("a_wo")
        ld_s, ld_qk, ld_v, ld_f = sem("ld_s"), sem("ld_qk"), sem("ld_v"), sem("ld_f")
        l_chr, l_chs, l_tab, l_kh, l_trs = sem("l_chr"), sem("l_chs"), sem("l_tab"), sem("l_kh"), sem("l_trs")
        l_xs, l_qk, l_v, l_sq, l_vc, l_qn, l_rb = (
            sem(n) for n in ("l_xs", "l_qk", "l_v", "l_sq", "l_vc", "l_qn", "l_rb"))
        l_ra, l_yq, l_yk, l_tr, l_trc, l_s, l_e, l_p = (
            sem(n) for n in ("l_ra", "l_yq", "l_yk", "l_tr", "l_trc", "l_s", "l_e", "l_p"))
        l_pt, l_ptc, l_pv, l_on, l_ot, l_oc, l_wo, l_res, l_xf, l_fn = (
            sem(n) for n in ("l_pt", "l_ptc", "l_pv", "l_on", "l_ot", "l_oc", "l_wo", "l_res", "l_xf", "l_fn"))
        f_h, f_g, f_hd, f_y = sem("f_h"), sem("f_g"), sem("f_hd"), sem("f_y")
        m_lg, m_sh, m_ex, m_oh, m_cum, m_ch, m_idx = (
            sem(n) for n in ("m_lg", "m_sh", "m_ex", "m_oh", "m_cum", "m_ch", "m_idx"))
        m_tk, m_tkc, m_zero, m_sc, m_xd = (sem(n) for n in ("m_tk", "m_tkc", "m_zero", "m_sc", "m_xd"))
        m_w, m_yo = [[sem(f"{n}{j}") for j in range(2)] for n in ("m_w", "m_yo")]
        m_d, m_dc, m_h, m_hc, m_y, m_yc, m_g = (
            sem(n) for n in ("m_d", "m_dc", "m_h", "m_hc", "m_y", "m_yc", "m_g"))
        m_xo, m_fin, m_out = sem("m_xo"), sem("m_fin"), sem("m_out")

        block = ctx.enter_context(nc.Block())

        def settle(eng):
            eng.sem_inc(settled, 1)

        def ln_mean_of(pe, src, b0):
            pe.matmul(bank[:, b0, :], mean_w[:, :], src, start=True, stop=True).then_inc(ln_mean, 1)

        def ln_var_of(pe, k, b1):
            pe.wait_ge(ln_sq, k + 1)
            pe.matmul(bank[:, b1, :], mean_w[:, :], sqn[:, :], start=True, stop=True).then_inc(ln_var, 1)

        def ln_centre(dve, k, src, b0):
            dve.wait_ge(ln_mean, k + 1)
            dve.tensor_tensor(xc[:, :], src, bank[:, b0, :], ALU.subtract).then_inc(ln_c, 1)

        def ln_scale(dve, k, dst):
            dve.wait_ge(ln_r, k + 1)
            dve.reciprocal(sqn[:, :], rstd[:, :]).then_inc(ln_i, 1)
            dve.wait_ge(ln_i, k + 1)
            dve.tensor_tensor(dst, xc[:, :], sqn[:, :], ALU.mult).then_inc(ln_out, 1)

        def ln_squares(act, k):
            act.wait_ge(ln_c, k + 1)
            act.activation(sqn[:, :], xc[:, :], ACT.Square).then_inc(ln_sq, 1)

        def ln_root(act, k, b1):
            act.wait_ge(ln_var, k + 1)
            act.activation(rstd[:, :], bank[:, b1, :], ACT.Sqrt, bias=eps[:, 0:1]).then_inc(ln_r, 1)

        def ln_scalar(act, k, b1):
            ln_squares(act, k)
            ln_root(act, k, b1)

        squares_all, roots_all = (big[:, j, :].rearrange("p (b t) -> p b t", b=BATCH) for j in range(2))

        def norm_all_tensor(pe, base):
            pe.wait_ge(step_done, base + 1)
            for b in range(BATCH):
                ln_mean_of(pe, xT[:, b, :], b)
            for b in range(BATCH):
                pe.wait_ge(ln_sq, base + b + 1)
                pe.matmul(bank[:, 4 + b, :], mean_w[:, :], squares_all[:, b, :], start=True, stop=True).then_inc(ln_var, 1)

        def norm_all_scalar(act, base):
            for b in range(BATCH):
                act.wait_ge(ln_c, base + b + 1)
                act.activation(squares_all[:, b, :], zT[:, b, :], ACT.Square).then_inc(ln_sq, 1)
            for b in range(BATCH):
                act.wait_ge(ln_var, base + b + 1)
                act.activation(roots_all[:, b, :], bank[:, 4 + b, :], ACT.Sqrt, bias=eps[:, 0:1]).then_inc(ln_r, 1)

        def norm_all_vector(dve, base):
            dve.wait_ge(step_done, base + 1)
            for b in range(BATCH):
                dve.wait_ge(ln_mean, base + b + 1)
                dve.tensor_tensor(zT[:, b, :], xT[:, b, :], bank[:, b, :], ALU.subtract).then_inc(ln_c, 1)
            for b in range(BATCH):
                dve.wait_ge(ln_r, base + b + 1)
                dve.reciprocal(roots_all[:, b, :], roots_all[:, b, :]).then_inc(ln_i, 1)
                dve.wait_ge(ln_i, base + b + 1)
                dve.tensor_tensor(zT[:, b, :], zT[:, b, :], roots_all[:, b, :], ALU.mult).then_inc(step_done, 1)
            dve.wait_ge(step_done, base + BATCH + 1)
            dve.sem_inc(ln_out, BATCH)

        const_loads = [
            (mean_w[:, :], I["c_mean"]), (ropeC[:, :, :], I["c_ropeC"]), (ropeS[:, :, :], I["c_ropeS"]),
            (packed_m[:, :], I["c_selm"]), (rotC[:, :, :], I["c_rotC"]), (rotS[:, :, :], I["c_rotS"]),
            (mask_f[:, 0:256], I["c_maskw"]), (mask_f[:, 256:768], I["c_maskr"]), (moe_c[:, :, :], I["c_moe"]),
            (upper[:, :], I["c_upper"]),
        ]

        gw = sb("gw", [P, NE])
        weight_loads = [
            (packed[:, :], I["packed"]), (packed_low[:, :], I["packed_low"]), (bias[:, :], I["bias_columns"]),
            (gw[:, :], I["gate_t"]),
        ]
        xrows = I["L0_attn_x"].rearrange("a (c p) d -> p (a c) d", p=P)
        LOADED = 16 * (len(const_loads) + len(weight_loads))
        SEED, LAYER0, ATT1, MOE0 = BATCH, 2 * BATCH, (2 + DEPTH) * BATCH, (3 + DEPTH) * BATCH
        WRITTEN = 16 * 2 * len(STACK)
        STACKED = 16 * 4
        LDF = 13 * 16

        @block.sync
        def _(sp):
            sp.dma_start(ident[:, :], I["c_ident"]).then_inc(ld_x, 16)
            sp.dma_start(big[:, 0, :].rearrange("p (a d) -> p a d", d=P), xrows).then_inc(ld_x, 16)
            for dst, src in const_loads + weight_loads:
                sp.dma_start(dst, src).then_inc(ld_c, 16)
            sp.wait_ge(zeros_set, 1)
            for j in range(5):
                sp.dma_start(disp[j * 512:(j + 1) * 512, :].rearrange("(p r) d -> p (r d)", r=4),
                             oTl[:, 0, :]).then_inc(m_zero, 16)

            def load_layer(l, first):
                if not first:
                    sp.wait_ge(l_tab, l * 3)
                    settle(sp)
                for j, name in enumerate(("L0_ffn_q_scale", "L0_ffn_k_scale")):
                    sp.dma_start(qks[:, j, :], I[name][l, :].rearrange("(o d) -> o d", o=1).broadcast_to([P, LD])).then_inc(ld_s, 16)
                if not first:
                    sp.wait_ge(l_qk, l * (TILES * BATCH))
                    settle(sp)
                sp.dma_start(wqkv[:, 0:2 * INNER], I["L0_ffn_Wqkv"][l, :, 0:2 * INNER]).then_inc(ld_qk, 16)
                if not first:
                    sp.wait_ge(l_v, l * (4 * TILES * BATCH))
                    settle(sp)
                sp.dma_start(wqkv[:, 2 * INNER:], I["L0_ffn_Wqkv"][l, :, 2 * INNER:]).then_inc(ld_v, 16)
                if not first:
                    sp.wait_ge(l_wo, l * BATCH)
                sp.dma_start(wol[:, :, :], I["L0_ffn_Wo"][l, :, :].rearrange("(a p) d -> p a d", p=P)).then_inc(ld_f, 16)
                if not first:
                    sp.wait_ge(step_done, l * BATCH + LAYER0 + 1)
                sp.dma_start(w1[:, :], I["L0_ffn_W1"][l, :, :]).then_inc(ld_f, 16)
                sp.dma_start(w2[:, 0:2, :], I["L0_ffn_W2"][l, 0:256, :].rearrange("(a p) d -> p a d", p=P)).then_inc(ld_f, 16)
                sp.dma_start(w2[0:FCH[2][1], 2, :], I["L0_ffn_W2"][l, 256:FF, :]).then_inc(ld_f, 16)
                for j, name in enumerate(("L0_ffn_ln_g", "L0_ffn_ln_b", "L0_ffn_b2")):
                    sp.dma_start(lb[:, j:j + 1], I[name][l, :].rearrange("(p o) -> p o", o=1)).then_inc(ld_f, 16)
                for j in range(6):
                    c0, n = FCH[j % 3]
                    c0 += FF * (j // 3)
                    sp.dma_start(lb[0:n, 3 + j:4 + j], I["L0_ffn_b1"][l, c0:c0 + n].rearrange("(p o) -> p o", o=1)).then_inc(ld_f, 16)

            for which in range(2):
                for r in range(2):
                    sp.dma_start(part_rows[which, MAX_ROW // AD, r], max_rows[which]).then_inc(a_one, 16)

            def stacks(a):
                sp.wait_ge(a_one, 4 * 16)
                sp.wait_ge(a_clr, 4 * a + 4)
                sp.wait_ge(zeros_set, 3 * a + 1)
                sp.wait_ge(m_zero, 5 * 16)
                with sp.Fori(0, BATCH) as b:
                    n = a * BATCH + b
                    for which in range(2):
                        sp.wait_ge((a_qf, a_kf)[which], 3 * n + 3)
                        settle(sp)
                        for c, row in enumerate(STACK_ROW):
                            sp.dma_start(part_rows[which, row // AD].rearrange("r d (p t) -> p (r d) t", t=SEQ),
                                         parts[:, 3 * which + STACK[c][which], :]).then_inc(a_scr, 16)
                    sp.wait_ge(a_scr, WRITTEN * n + WRITTEN)
                    settle(sp)
                    sp.wait_ge(a_last, n + 1)
                    settle(sp)
                    for which in (1, 0):
                        for r in range(2):
                            o = 64 * r
                            dst = qst2[o:o + SROWS, r, :] if which == 0 else kst2[o:o + SROWS, :]
                            sp.dma_start(dst, part_rows[which, :, r]).then_inc(a_stk, 16)
                    sp.wait_ge(a_stk, STACKED * n + STACKED)
                    settle(sp)

            load_layer(0, True)
            stacks(0)
            with sp.Fori(1, DEPTH) as l:
                load_layer(l, False)
            stacks(1)
            sp.wait_ge(step_done, ATT1 + 1)
            for e in range(NE):
                if e >= 2:
                    sp.wait_ge(m_h, e - 1)
                    sp.wait_ge(m_y, e - 1)
                sp.dma_start(ew1[:, e % 2, :], I["L1_ffn_w1"][e]).then_inc(m_w[e % 2], 16)
                sp.dma_start(ew2[:, e % 2, :, :], I["L1_ffn_w2"][e].rearrange("(f p) d -> p f d", p=P)).then_inc(m_w[e % 2], 16)
            sp.wait_ge(m_fin, 4)
            sp.dma_start(out.rearrange("a (c p) d -> p (a c) d", p=P), fin).then_inc(m_out, 16)
            sp.wait_ge(m_out, 16)

        @block.gpsimd
        def _(pool):
            pool.memset(oTl[:, :, :], 0.0).then_inc(zeros_set, 1)
            pool.memset(xs[:, 0, 0:WIN + 1], 0.0).then_inc(init, 1)
            pool.memset(xs[:, 1, 0:WIN + 1], 0.0).then_inc(init, 1)
            pool.memset(eps[:, :], EPS).then_inc(init, 1)
            pool.sem_inc(a_last, 1)
            def clear():
                pool.memset(vbuf[:, 0:2048], 0.0).then_inc(a_clr, 1)
                pool.memset(nmp, 0.0).then_inc(a_clr, 1)
                pool.memset(va[:, :, :, AD + 1:], 0.0).then_inc(a_clr, 1)
                pool.memset(va[:, :, :, AD:AD + 1], 1.0).then_inc(a_clr, 1)

            clear()
            pool.wait_ge(step_done, LAYER0 + 1)
            pool.memset(vbuf[:, :], 0.0).then_inc(zeros_set, 1)
            pool.memset(kflat, 0.0).then_inc(zeros_set, 1)
            pool.sem_inc(l_trs, 1)
            with pool.Fori(0, DEPTH) as l:
                pool.wait_ge(l_tab, l * 3 + 3)
                settle(pool)
                with pool.Fori(0, BATCH) as b:
                    for i in range(TILES):
                        T = (l * BATCH + b) * TILES + i
                        pool.wait_ge(l_qn, T + 1)
                        pool.wait_ge(l_trs, T + 1)
                        q4 = qn.rearrange("p (a h d) -> p a h d", a=2, h=LH)
                        r4 = rotB.rearrange("p (a h d) -> p a h d", a=2, h=LH)
                        tab = rotSl[:, i, :].rearrange("p (a d) -> p a d", a=2).unsqueeze(2).broadcast_to([P, 2, LH, LD])
                        h = LD // 2
                        pool.tensor_tensor(r4[:, :, :, 0:h], q4[:, :, :, h:], tab[:, :, :, 0:h], ALU.mult).then_inc(l_rb, 1)
                        pool.tensor_tensor(r4[:, :, :, h:], q4[:, :, :, 0:h], tab[:, :, :, h:], ALU.mult).then_inc(l_rb, 1)
                        pool.wait_ge(l_ra, T + 1)
                        pool.wait_ge(l_rb, 2 * T + 2)
                        pool.tensor_tensor(rotB[:, INNER:], rotA[:, INNER:], rotB[:, INNER:], ALU.add).then_inc(l_yk, 1)
                        if i + 1 < TILES:
                            pool.wait_ge(l_trc, 3 * T + 3)
                            settle(pool)
                            pool.tensor_copy(kD[:, (i + 1) % 2, :, :, 0:WIN], kD[:, i % 2, :, :, P:P + WIN]).then_inc(l_kh, 1)
            pool.wait_ge(step_done, ATT1 + 1)
            pool.memset(oTl[:, :, :], 0.0).then_inc(zeros_set, 1)
            pool.memset(ones, 1.0).then_inc(zeros_set, 1)
            clear()
            pool.wait_ge(m_zero, 5 * 16)
            pool.wait_ge(m_idx, 2)
            pool.wait_ge(m_tkc, 4)
            for i in range(NT):
                pool.indirect_dma_start(disp, bass.IndirectOffsetOnAxis(ap=idx[:, 0, i:i + 1], axis=0),
                                        xtok[:, i, :], None).then_inc(m_sc, 16)
            pool.wait_ge(m_sc, 16 * NT)
            pool.dma_start(xd, disp[0:SLOTS, :].rearrange("(a p) d -> p a d", p=HC)).then_inc(m_xd, 16)
            for e in range(NE):
                pool.wait_ge(m_yc, e + 1)
                pool.dma_start(yrow[e * CAP:(e + 1) * CAP, :].rearrange("(c p) d -> p c d", p=HC),
                               yo[:, e % 2, :, :]).then_inc(m_yo[e % 2], 16)
            for j in range(2):
                pool.wait_ge(m_yo[j], 16 * NE // 2)
            for i in range(NT):
                pool.indirect_dma_start(gat[:, i, :], None, yrow,
                                        bass.IndirectOffsetOnAxis(ap=idx[:, 1, i:i + 1], axis=0)).then_inc(m_g, 16)

        @block.tensor
        def _(pe):
            pe.wait_ge(ld_x, 32)
            xin = big[:, 0, :].rearrange("p (a d) -> p a d", d=P)
            for b in range(BATCH):
                for c in range(TILES):
                    t = pe.transpose(bank[:, b, c * P:(c + 1) * P], xin[:, b * TILES + c, :], ident[:, :])
                t.then_inc(x_tr, 1)
            pe.wait_ge(ld_c, LOADED)
            pe.wait_ge(x_in, BATCH)

            def lead(a, b, step):
                k = (ATT1 if a else 0) + b
                todo = projections(a)
                if step == 0:
                    ln_mean_of(pe, xT[:, b, :], 6)
                elif step == 1:
                    ln_var_of(pe, k, 7)
                else:
                    e = step - 2
                    if e == 0:
                        pe.wait_ge(ln_out, k + 1)
                    if e >= 2:
                        pe.wait_ge(a_raw[a], b * (len(todo) + 1) + e - 1)
                    if e < len(todo):
                        w, src, dst, _ = todo[e]
                        m = pe.matmul(bank[0:w.shape[1], 6 + e % 2, :], w, src, start=True, stop=True)
                    else:
                        for c in range(TILES):
                            src, w = (ckv, wuv[:, :]) if a == 0 else (xn[:, :], wv1[:, :])
                            m = pe.matmul(bank[:, 6 + e % 2, c * P:(c + 1) * P], src[:, c * P:(c + 1) * P], w,
                                          start=True, stop=True)
                    m.then_inc(a_prj[a], 1)

            def attention(a):
                base = ATT1 if a else 0
                pe.wait_ge(step_done, base + 1)
                for step in range(len(LEAD[a])):
                    lead(a, 0, step)
                with pe.Fori(0, BATCH - 1) as b:
                    batch(a, b, True)
                batch(a, BATCH - 1, False)

            def batch(a, b, follow):
                base = ATT1 if a else 0
                k, n = base + b, a * BATCH + b
                pe.wait_ge(a_stk, STACKED * n + STACKED)
                pe.wait_ge(step_done, k + 1)
                pe.wait_ge(a_raw[a], (b + 1) * (len(LEAD[a]) - 2))

                for u in range(MUNITS):
                    qt, p = divmod(u, PAIRS_A)
                    if u >= 3:
                        pe.wait_ge(a_mx, n * MUNITS + u - 2)
                    for r in range(2):
                        m = pe.matmul(bank[:, 2 * (u % 3) + r, :], qst[:, p, r, qt * P:(qt + 1) * P],
                                      kst[:, p, :], start=True, stop=True)
                    m.then_inc(a_s, 1)
                    if follow and u in LEAD[a]:
                        lead(a, b + 1, LEAD[a].index(u))
                pe.wait_ge(a_nm, n + 1)
                for qt in range(TILES):
                    t = pe.transpose(bank[:, 0, qt * P:(qt + 1) * P], nmp[:, qt, :], ident[:, :])
                t.then_inc(a_t, 1)
                pe.wait_ge(a_tc, n + 1)
                if follow:
                    pe.wait_ge(a_raw[a], (b + 2) * (len(LEAD[a]) - 2))
                for half in range(2):
                    for p in range(4 * half, 4 * half + 4):
                        for r in range(2):
                            h = 2 * p + r
                            m = pe.matmul(bank[64 * r + MAX_ROW:64 * r + MAX_ROW + 32, p, :], sel_m[:, 32 * h:32 * h + 32], nmT,
                                          start=True, stop=True, tile_position=(0, 64 * r + MAX_ROW), skip_group_check=True)
                    m.then_inc(a_sm, 1)
                pe.wait_ge(a_me, 2 * n + 1)
                pe.wait_ge(a_mo, 2 * n + 1)

                def scores_t(i):
                    u, half = divmod(i, 2)
                    j, kt = divmod(u, TILES)
                    if i == 2:
                        pe.wait_ge(a_me, 2 * n + 2)
                        pe.wait_ge(a_mo, 2 * n + 2)
                    if i >= 3:
                        pe.wait_ge(a_p, n * PAIRQ + i - 2)
                    for r in range(2):
                        m = pe.matmul(bank[:, 2 * (i % 3) + r, :], kst[:, 2 * j + half, kt * P:(kt + 1) * P],
                                      qst[:, 2 * j + half, r, :], start=True, stop=True)
                    m.then_inc(a_st, 1)

                scores_t(0)
                scores_t(1)
                for u in range(UNITS):
                    if u + 1 < UNITS:
                        scores_t(2 * u + 2)
                        scores_t(2 * u + 3)
                    j, kt = divmod(u, TILES)
                    pe.wait_ge(a_p, n * PAIRQ + 2 * u + 2)
                    if u == 0:
                        pe.wait_ge(a_vc, n + 1)
                    if u == UNITS - 1:
                        pe.wait_ge(a_st, n * PAIRQ + PAIRQ)
                        pe.sem_inc(a_last, 1)
                    if kt == 0 and j >= 2:
                        pe.wait_ge(a_oc, n * HG + j - 1)
                    for g in range(4):
                        m = pe.matmul(bank[32 * g:32 * g + AV, 6 + j % 2, :], va[:, kt, HG * j + g, :],
                                      pT[:, u % 2, g, :], start=(kt == 0), stop=(kt == TILES - 1),
                                      tile_position=(0, 32 * g))
                    m.then_inc(a_pv, 1)
                pe.wait_ge(a_oc, HG * (n + 1))
                for qt in range(TILES):
                    for j in range(HG):
                        t = pe.transpose(bank[:, qt, j * P:(j + 1) * P], oU[:, j, qt * P:(qt + 1) * P], ident[:, :])
                    t.then_inc(a_ob, 1)
                for qt in range(TILES):
                    pe.wait_ge(a_on, n * TILES + qt + 1)
                    pe.transpose(bank[:, 4, qt * P:(qt + 1) * P], on[:, qt % 2, :], ident[:, :]).then_inc(a_ot, 1)
                pe.wait_ge(a_otc, n + 1)
                pe.matmul(bank[:, 5, :], wo[:, a, :], oT, start=True, stop=True).then_inc(a_wo, 1)

            attention(0)

            norm_all_tensor(pe, SEED)

            def project_qk(it, b, i, tail):
                T = it * TILES + i
                x = xs[:, (b + i // TILES) % 2, :]
                if i == TILES:
                    pe.wait_ge(l_xs, 2 * it + 4)
                    if b == BATCH - 1:
                        pe.wait_ge(ld_qk, it * 4 + 20)
                if not (b == 0 and i == 0):
                    pe.wait_ge(l_qn, T)
                if tail and i == 2:
                    pe.wait_ge(l_res, it)
                if tail and i == 3:
                    pe.wait_ge(ln_r, LAYER0 + it)
                if tail and i >= 4:
                    pe.wait_ge(f_hd, 3 * it + i - 5)
                s = WIN + (i % TILES) * P
                for c in range(4):
                    m = pe.matmul(bank[:, c, :], x[:, s:s + P],
                                  wqkv[:, c * 512:(c + 1) * 512], start=True, stop=True)
                m.then_inc(l_qk, 1)

            def project_v(it, b, i, tail):
                T = it * TILES + i
                x = xs[:, (b + i // TILES) % 2, :]
                wv = wqkv[:, 2 * INNER:].rearrange("p (a r d) -> p r a d", r=2, d=LD)
                if i == TILES and b == BATCH - 1:
                    pe.wait_ge(ld_v, it * 4 + 20)
                if i >= 1:
                    pe.wait_ge(l_ptc, T)
                for w in range(4):
                    if tail and w == 1 and i == 1:
                        pe.wait_ge(ln_c, LAYER0 + it)
                    if tail and w == 1 and i == TILES:
                        pe.wait_ge(step_done, LAYER0 + it + 1)
                    if w >= 2:
                        pe.wait_ge(l_vc, 8 * T + 2 * (w - 1))
                    s = (i % TILES) * P + w * WIN
                    for r in range(2):
                        m = pe.matmul(bank[64 * r:64 * r + 64, 6 + w % 2, :], x[:, s:s + 2 * WIN],
                                      wv[:, r, :, :], start=True, stop=True)
                    m.then_inc(l_v, 1)

            def turn_q(T):
                if not (isinstance(T, int) and T == 0):
                    pe.wait_ge(l_on, T)
                pe.wait_ge(l_yq, T + 1)
                for c in range(PAIRS):
                    t = pe.transpose(bank[:, 4 + c // 4, (c % 4) * P:(c % 4 + 1) * P], rotB[:, c * P:(c + 1) * P], ident[:, :])
                t.then_inc(l_tr, 1)

            def tiles(l, b, tail, follow):
                it = l * BATCH + b

                def turn_k(i):
                    T = it * TILES + i
                    if i >= 1 or tail:
                        pe.wait_ge(l_oc, T)
                    else:
                        pe.wait_ge(l_vc, 8)
                    pe.wait_ge(l_yk, T + 1)
                    for c in range(PAIRS):
                        t = pe.transpose(bank[:, 6 + c // 4, (c % 4) * P:(c % 4 + 1) * P],
                                         rotB[:, INNER + c * P:INNER + (c + 1) * P], ident[:, :])
                    t.then_inc(l_trs, 1)

                def scores(i):
                    T = it * TILES + i
                    pe.wait_ge(l_trc, 3 * T + 1)
                    settle(pe)
                    for a in range(2):
                        pe.matmul(bank[:, 4 + a, :], maskw[:, min(i, 1), :], maskr[:, :], start=True, stop=False,
                                  skip_group_check=True)
                    pe.wait_ge(l_trc, 3 * T + 3)
                    if i >= 1:
                        pe.wait_ge(l_kh, it * (TILES - 1) + i)
                    settle(pe)
                    for c in range(PAIRS):
                        for w in range(4):
                            m = pe.matmul(bank[32 * w:32 * w + 32, 4 + c // 4, (c % 4) * P:(c % 4 + 1) * P],
                                          qT[:, i % 2, c, w * WIN:(w + 1) * WIN],
                                          kD[:, i % 2, c, :, w * WIN:(w + 2) * WIN], start=False, stop=True,
                                          tile_position=(0, 32 * w), skip_group_check=True)
                    m.then_inc(l_s, 1)

                def turn_p(i):
                    T = it * TILES + i
                    pe.wait_ge(l_p, T + 1)
                    for c in range(PAIRS):
                        t = pe.transpose(bank[:, 6 + c // 4, (c % 4) * P:(c % 4 + 1) * P], sc[:, 1, c * P:(c + 1) * P], ident[:, :])
                    t.then_inc(l_pt, 1)

                def weigh(i):
                    T = it * TILES + i
                    pe.wait_ge(l_vc, 8 * T + 8)
                    pe.wait_ge(l_ptc, T + 1)
                    pe.wait_ge(l_e, T + 1)
                    settle(pe)
                    for c in range(PAIRS):
                        for w in range(4):
                            m = pe.matmul(bank[32 * w:32 * w + 32, 4 + c // 4, (c % 4) * P:(c % 4 + 1) * P],
                                          sc[:, 3, c * P + w * WIN:c * P + (w + 1) * WIN], vD[:, w, c, :, :],
                                          start=True, stop=True, tile_position=(0, 32 * w))
                    m.then_inc(l_pv, 1)

                def turn_o(i):
                    T = it * TILES + i
                    pe.wait_ge(l_on, T + 1)
                    if i + 1 < TILES or follow:
                        pe.wait_ge(l_vc, 8 * T + 16)
                    else:
                        pe.wait_ge(l_ptc, T + 1)
                        pe.wait_ge(step_done, LAYER0 + it + 1)
                    for c in range(PAIRS):
                        t = pe.transpose(bank[:, 6 + c // 4, (c % 4) * P:(c % 4 + 1) * P], sc[:, 2, c * P:(c + 1) * P], ident[:, :])
                    t.then_inc(l_ot, 1)

                if tail and b == 1:
                    pe.wait_ge(ld_f, (it - 1) * (LDF // BATCH) + LDF)
                for i in range(TILES):
                    turn_k(i)
                    if tail:
                        pe.wait_ge(l_qn, it * TILES + (i + 2 if i + 1 < TILES or follow else TILES))
                        (project_out, ffn_var, ffn_in, ffn_in_last)[i](it - 1)
                    scores(i)
                    if i + 2 < TILES or follow:
                        project_qk(it, b, i + 2, tail)
                    turn_p(i)
                    weigh(i)
                    if tail and i == 0:
                        ffn_mean(it - 1)
                    if tail and i == TILES - 1:
                        ffn_out(it - 1)
                    if i + 1 < TILES or follow:
                        project_v(it, b, i + 1, tail)
                        turn_q(it * TILES + i + 1)
                    turn_o(i)

            def project_out(it):
                pe.wait_ge(l_oc, (it + 1) * TILES)
                for c in range(PAIRS):
                    m = pe.matmul(bank[:, 0, :], wol[:, c, :], oTl[:, c, :], start=(c == 0), stop=(c == PAIRS - 1))
                m.then_inc(l_wo, 1)

            def ffn_mean(it):
                pe.wait_ge(l_xf, 3 * it + 3)
                ln_mean_of(pe, xf, 7)

            def ffn_var(it):
                ln_var_of(pe, LAYER0 + it, 0)

            def ffn_in(it):
                pe.wait_ge(l_fn, it + 1)
                for j in range(2):
                    c0, n = FCH[j]
                    pe.matmul(bank[0:n, 2 * j, :], w1[:, FF + c0:FF + c0 + n], xn[:, :], start=True, stop=True).then_inc(f_h, 1)
                    pe.matmul(bank[0:n, 2 * j + 1, :], w1[:, c0:c0 + n], xn[:, :], start=True, stop=True).then_inc(f_h, 1)

            def ffn_in_last(it):
                c0, n = FCH[2]
                pe.wait_ge(f_hd, 3 * it + 1)
                pe.matmul(bank[0:n, 0, :], w1[:, FF + c0:FF + c0 + n], xn[:, :], start=True, stop=True).then_inc(f_h, 1)
                pe.matmul(bank[0:n, 1, :], w1[:, c0:c0 + n], xn[:, :], start=True, stop=True).then_inc(f_h, 1)

            def ffn_out(it):
                for j in range(3):
                    pe.wait_ge(f_hd, 3 * it + j + 1)
                    n = FCH[j][1]
                    m = pe.matmul(bank[:, 7, :], w2[0:n, j, :], hT[0:n, j, :], start=(j == 0), stop=(j == 2))
                m.then_inc(f_y, 1)

            pe.wait_ge(ld_qk, 16)
            pe.wait_ge(ld_v, 16)
            pe.wait_ge(zeros_set, 3)
            pe.wait_ge(step_done, LAYER0 + 1)
            pe.wait_ge(l_xs, 2)
            project_qk(0, 0, 0, False)
            project_v(0, 0, 0, False)
            project_qk(0, 0, 1, False)
            turn_q(0)
            tiles(0, 0, False, True)
            with pe.Fori(0, DEPTH - 1) as l:
                for b in range(1, BATCH):
                    tiles(l, b, True, True)
                tiles(l + 1, 0, True, True)
            for b in range(1, BATCH):
                tiles(DEPTH - 1, b, True, b + 1 < BATCH)
            last = DEPTH * BATCH - 1
            project_out(last)
            ffn_mean(last)
            ffn_var(last)
            pe.wait_ge(ln_r, LAYER0 + last + 1)
            ffn_in(last)
            ffn_in_last(last)
            ffn_out(last)

            pe.wait_ge(x_sum, BATCH)
            attention(1)

            norm_all_tensor(pe, MOE0)
            pe.wait_ge(step_done, MOE0 + BATCH + 1)
            zf = zT[:, :, :].rearrange("p b t -> p (b t)")
            for i in range(NT):
                m = pe.matmul(bank[:, 2, i * NE:(i + 1) * NE], zf[:, i * P:(i + 1) * P], gw[:, :], start=True, stop=True)
            m.then_inc(m_lg, 1)
            for i in range(NT):
                t = pe.transpose(bank[:, 3 + i // 4, (i % 4) * P:(i % 4 + 1) * P], zf[:, i * P:(i + 1) * P], ident[:, :])
            t.then_inc(m_tk, 1)
            pe.wait_ge(m_oh, 1)
            pe.wait_ge(zeros_set, 5)
            pe.matmul(bank[:, 7, 0:256], upper[:, :], rt[:, 3, :], start=True, stop=True)
            pe.matmul(bank[:, 0, 0:256], ones, rt[:, 3, :], start=True, stop=True).then_inc(m_cum, 1)
            pe.wait_ge(m_idx, 2)
            pe.wait_ge(m_tkc, 4)
            pe.wait_ge(m_xd, 16)

            def bring(e):
                if e >= 2:
                    pe.wait_ge(m_dc, e - 1)
                for c in range(2):
                    t = pe.transpose(bank[:, e % 2, c * HC:(c + 1) * HC], xd[:, 2 * e + c, :], ident[0:HC, 0:HC])
                t.then_inc(m_d, 1)

            def hidden(e):
                pe.wait_ge(m_dc, e + 1)
                pe.wait_ge(m_w[e % 2], 32 * (e // 2 + 1))
                if e >= 2:
                    pe.wait_ge(m_hc, 2 * e - 2)
                for f in range(4):
                    m = pe.matmul(bank[:, (2, 6)[e % 2] + f // 2, (f % 2) * CAP:(f % 2 + 1) * CAP], ew1[:, e % 2, f * P:(f + 1) * P],
                                  dT[:, e % 2, :], start=True, stop=True)
                m.then_inc(m_h, 1)

            bring(0)
            bring(1)
            hidden(0)
            for e in range(NE):
                if e + 1 < NE:
                    hidden(e + 1)
                if e + 2 < NE:
                    bring(e + 2)
                pe.wait_ge(m_hc, 2 * e + 2)
                if e >= 2:
                    pe.wait_ge(m_yc, e - 1)
                for c in range(2):
                    for f in range(4):
                        m = pe.matmul(bank[0:HC, 4 + e % 2, c * P:(c + 1) * P], eh[:, e % 2, f // 2, f % 2, c * HC:(c + 1) * HC],
                                      ew2[:, e % 2, f, :], start=(f == 0), stop=(f == 3))
                m.then_inc(m_y, 1)
            pe.wait_ge(m_yc, NE)
            xflat = xT[:, :, :].rearrange("p b t -> p (b t)")
            for q in range(4):
                for i in range(4 * q, 4 * q + 4):
                    t = pe.transpose(bank[:, (6, 7, 0, 1)[q], (i % 4) * P:(i % 4 + 1) * P], xflat[:, i * P:(i + 1) * P], ident[:, :])
                t.then_inc(m_xo, 1)

        @block.scalar
        def _(act):
            def lead(a, b):
                ln_scalar(act, (ATT1 if a else 0) + b, 7)
                todo = projections(a)
                for e in range(len(todo) + 1):
                    act.wait_ge(a_prj[a], b * (len(todo) + 1) + e + 1)
                    if e < len(todo):
                        _, _, dst, shift = todo[e]
                        act.activation(dst, bank[0:dst.shape[0], 6 + e % 2, :], ACT.Identity, bias=shift).then_inc(a_raw[a], 1)
                    else:
                        act.activation(vraw, bank[:, 6 + e % 2, :], ACT.Copy).then_inc(a_raw[a], 1)

            def attention(a):
                act.wait_ge(step_done, (ATT1 if a else 0) + 1)
                lead(a, 0)
                with act.Fori(0, BATCH - 1) as b:
                    batch(a, b, True)
                batch(a, BATCH - 1, False)

            def batch(a, b, follow):
                base = ATT1 if a else 0
                k, n = base + b, a * BATCH + b
                act.wait_ge(a_raw[a], (b + 1) * (len(LEAD[a]) - 2))
                act.wait_ge(step_done, k + 1)
                act.wait_ge(a_clr, 4 * a + 4)
                act.activation(va[:, :, :, 0:AD], vraw.rearrange("p (c h d) -> p c h d", c=TILES, h=AH),
                               ACT.Copy).then_inc(a_vc, 1)
                if follow:
                    act.wait_ge(a_vc, n + 1)
                    lead(a, b + 1)
                act.wait_ge(a_t, n + 1)
                act.activation(nmT, bank[:, 0, :], ACT.Copy).then_inc(a_tc, 1)
                for half in range(2):
                    act.wait_ge(a_sm, 2 * n + half + 1)
                    act.activation(qst[MAX_ROW:MAX_ROW + 3, 4 * half:4 * half + 4, 0, :],
                                   bank[MAX_ROW:MAX_ROW + 3, 4 * half:4 * half + 4, :], ACT.Copy).then_inc(a_me, 1)
                for i in range(PAIRQ):
                    act.wait_ge(a_st, n * PAIRQ + i + 1)
                    u, half = divmod(i, 2)
                    if u >= 2:
                        act.wait_ge(a_pv, n * UNITS + u - 1)
                    q = 2 * (i % 3)
                    act.activation(pT[:, u % 2, 2 * half:2 * half + 2, :], bank[:, q:q + 2, :], ACT.Exp).then_inc(a_p, 1)
                act.wait_ge(a_ot, (n + 1) * TILES)
                act.activation(oT, bank[:, 4, :], ACT.Identity,
                               bias=bias[:, 8 + 6 * a:9 + 6 * a]).then_inc(a_otc, 1)

            for b in range(BATCH):
                act.wait_ge(x_tr, b + 1)
                act.activation(xT[:, b, :], bank[:, b, :], ACT.Copy).then_inc(x_in, 1)
            act.wait_ge(ld_c, LOADED)
            act.wait_ge(init, 3)
            attention(0)
            norm_all_scalar(act, SEED)

            def shifted(it, b):
                act.activation(xs[0:64, b % 2, WIN:], zT[0:64, b, :], ACT.Copy).then_inc(l_xs, 1)

            def squares(T):
                act.wait_ge(l_qk, T + 1)
                act.activation(sq, bank[:, 0:4, :].rearrange("p a t -> p (a t)"), ACT.Square).then_inc(l_sq, 1)

            def values(T):
                for w in range(4):
                    act.wait_ge(l_v, 4 * T + w + 1)
                    for r in range(2):
                        act.activation(vD[64 * r:64 * r + 64, w, :, r, :],
                                       bank[64 * r:64 * r + 64, 6 + w % 2, :].rearrange("p (c d) -> p c d", d=LD),
                                       ACT.Copy).then_inc(l_vc, 1)

            def queries(T, i):
                act.wait_ge(l_tr, T + 1)
                act.activation(qT[:, i % 2, :, :], bank[:, 4:6, :].rearrange("p a (c t) -> p (a c) t", t=P), ACT.Copy).then_inc(l_trc, 1)

            def tiles(l, b, tail, follow):
                it = l * BATCH + b
                for i in range(TILES):
                    T = it * TILES + i
                    act.wait_ge(l_trs, T + 2)
                    settle(act)
                    for r in range(2):
                        act.activation(kD[64 * r:64 * r + 64, i % 2, :, r, WIN:],
                                       bank[64 * r:64 * r + 64, 6:8, :].rearrange("p a (c t) -> p (a c) t", t=P), ACT.Copy).then_inc(l_trc, 1)
                    if tail and i == 0:
                        shift_half(it - 1, (b - 1) % BATCH)
                    if tail and i == 1:
                        ln_root(act, LAYER0 + it - 1, 0)
                    if tail and i == 2:
                        gate(it - 1, 0)
                        gate(it - 1, 1)
                    if tail and i == 3:
                        gate(it - 1, 2)
                    act.wait_ge(l_e, T + 1)
                    act.activation(sc[:, 1, :], sc[:, 0, :], ACT.Exp, scale=8.0).then_inc(l_p, 1)
                    act.wait_ge(l_pt, T + 1)
                    act.activation(sc[:, 3, :], bank[:, 6:8, :].rearrange("p a t -> p (a t)"), ACT.Copy).then_inc(l_ptc, 1)
                    if i == 1 and follow:
                        if tail:
                            act.wait_ge(l_v, 4 * TILES * it)
                            settle(act)
                        act.wait_ge(step_done, LAYER0 + it + (0 if tail else 1))
                        settle(act)
                        shifted(it, (b + 1) % BATCH)
                    if i + 2 < TILES or follow:
                        squares(T + 2)
                    if i + 1 < TILES or follow:
                        act.wait_ge(l_pv, T + 1)
                        settle(act)
                        values(T + 1)
                    if tail and i == 0:
                        ln_squares(act, LAYER0 + it - 1)
                    if i + 1 < TILES or follow:
                        queries(T + 1, i + 1)
                    act.wait_ge(l_ot, T + 1)
                    act.activation(oTl[:, :, i * P:(i + 1) * P],
                                   bank[:, 6:8, :].rearrange("p a (c t) -> p (a c) t", t=P), ACT.Copy).then_inc(l_oc, 1)

            def shift_half(it, b):
                act.wait_ge(l_res, it + 1)
                settle(act)
                act.activation(xf[0:64, :], zT[0:64, b, :], ACT.Copy).then_inc(l_xf, 1)

            def gate(it, j):
                n = FCH[j][1]
                act.wait_ge(f_h, 6 * it + 2 * j + 1)
                act.activation(gates[0:n, j, :], bank[0:n, 2 * (j % 2), :], ACT.Gelu, bias=lb[0:n, 6 + j:7 + j]).then_inc(f_g, 1)

            act.wait_ge(zeros_set, 3)
            act.wait_ge(step_done, LAYER0 + 1)
            shifted(0, 0)
            squares(0)
            values(0)
            squares(1)
            queries(0, 0)
            tiles(0, 0, False, True)
            act.wait_ge(ld_f, LDF)
            with act.Fori(0, DEPTH - 1) as l:
                for b in range(1, BATCH):
                    tiles(l, b, True, True)
                tiles(l + 1, 0, True, True)
            for b in range(1, BATCH):
                tiles(DEPTH - 1, b, True, b + 1 < BATCH)
            last = DEPTH * BATCH - 1
            shift_half(last, BATCH - 1)
            ln_scalar(act, LAYER0 + last, 0)
            for j in range(3):
                gate(last, j)
            attention(1)
            norm_all_scalar(act, MOE0)
            act.wait_ge(m_tk, 1)
            for q in range(4):
                act.activation(xtok[:, 4 * q:4 * q + 4, :], bank[:, 3 + q, :].rearrange("p (a d) -> p a d", d=P), ACT.Copy).then_inc(m_tkc, 1)
            act.wait_ge(m_sh, 1)
            act.activation(rt[:, 1, :], rt[:, 0, :], ACT.Exp).then_inc(m_ex, 1)
            for e in range(NE):
                act.wait_ge(m_h, e + 1)
                if e >= 2:
                    act.wait_ge(m_y, e - 1)
                for r in range(2):
                    act.activation(eh[:, e % 2, r, :, :], bank[:, (2, 6)[e % 2] + r, 0:2 * CAP].rearrange("p (c t) -> p c t", c=2),
                                   ACT.Gelu_apprx_tanh).then_inc(m_hc, 1)

        def out_rows(dve, e):
            dve.wait_ge(m_y, e + 1)
            if e >= 2:
                dve.wait_ge(m_yo[e % 2], 16 * (e // 2))
            dve.tensor_copy(yo[:, e % 2, :, :], bank[0:HC, 4 + e % 2, 0:2 * P].rearrange("p (c d) -> p c d", c=2)).then_inc(m_yc, 1)

        @block.vector
        def _(dve):
            NEWTON = 2 + 3 * 3

            def inverse_root(ch, out, s):
                u = small[:, 5, :]
                ch.link(dve.tensor_scalar(s, s, 1e-24, None, ALU.max))
                ch.link(dve.tensor_scalar(out.bitcast(I32), s.bitcast(I32), -0.5, float(0x5F3759DF), ALU.mult, ALU.add))
                for _ in range(3):
                    ch.link(dve.scalar_tensor_tensor(out=u, in0=s, scalar=-0.5, in1=out, op0=ALU.mult, op1=ALU.mult))
                    ch.link(dve.tensor_tensor(u, u, out, ALU.mult))
                    ch.link(dve.scalar_tensor_tensor(out=out, in0=u, scalar=1.5, in1=out, op0=ALU.add, op1=ALU.mult))

            def rope(a, b, which):
                n = a * BATCH + b
                ch = Chain(dve, (a_ch, a_ch1)[a], b * (11 - 2 * a) + which * (6 - a))
                dst = (qf, kf)[which]
                plain, swap, up = (raw[:, 3 * which + j, :] for j in range(3))
                dve.wait_ge(a_raw[a], (b + 1) * (len(LEAD[a]) - 2))
                ch.link(dve.tensor_tensor(tA, plain, ropeC[:, a, :], ALU.mult))
                ch.link(dve.tensor_tensor(tB, swap, ropeS[:, a, :], ALU.mult))
                if a == 0:
                    ch.link(dve.tensor_tensor(tA, tA, tB, ALU.add))
                    ch.link(dve.tensor_tensor(dst, up, tA, ALU.add))
                else:
                    ch.link(dve.tensor_tensor(dst, tA, tB, ALU.add))
                if which == 0:
                    ch.link(dve.tensor_scalar(dst, dst, 1.0 / SCALE[a], None, ALU.mult))
                if which == 0 and not (isinstance(n, int) and n == 0):
                    dve.wait_ge(a_scr, WRITTEN * n)
                high, middle, low = (parts[:, 3 * which + p, :] for p in range(3))
                done = (a_qf, a_kf)[which]
                dve.tensor_copy(high, dst).then_inc(done, 1)
                dve.wait_ge(done, 3 * n + 1)
                ch.link(dve.tensor_tensor(tC, dst, high, ALU.subtract))
                dve.tensor_copy(middle, tC).then_inc(done, 1)
                dve.wait_ge(done, 3 * n + 2)
                dve.tensor_tensor(low, tC, middle, ALU.subtract).then_inc(done, 1)

            def attention(a):
                base = ATT1 if a else 0
                dve.wait_ge(step_done, base + 1)
                ln_centre(dve, base, xT[:, 0, :], 6)
                ln_scale(dve, base, xn[:, :])
                rope(a, 0, 0)
                rope(a, 0, 1)
                with dve.Fori(0, BATCH - 1) as b:
                    batch(a, b, True)
                batch(a, BATCH - 1, False)

            def batch(a, b, follow):
                base = ATT1 if a else 0
                k, n = base + b, a * BATCH + b
                ch = Chain(dve, a_chm, n * 5)
                dve.wait_ge(a_clr, 4 * a + 4)
                for u in range(MUNITS):
                    qt, p = divmod(u, PAIRS_A)
                    dve.wait_ge(a_s, n * MUNITS + u + 1)
                    dve.tensor_reduce(nm[:, qt, 2 * p:2 * p + 2], bank[:, 2 * (u % 3):2 * (u % 3) + 2, :], AX.X, ALU.max,
                                      negate=True).then_inc(a_mx, 1)
                    if follow and u == LEAD[a][0] + 2:
                        ln_centre(dve, k + 1, xT[:, b + 1, :], 6)
                    if follow and u == LEAD[a][1] + 3:
                        ln_scale(dve, k + 1, xn[:, :])
                dve.wait_ge(a_mx, n * MUNITS + MUNITS)
                ch.link(dve.tensor_copy(nmb, nm))
                ch.link(dve.tensor_copy(nmp[:, :, 0:AH], nmb))
                ch.link(dve.tensor_tensor(nmr, nm, nmb, ALU.subtract))
                ch.link(dve.tensor_copy(nmb, nmr))
                ch.link(dve.tensor_copy(nmp[:, :, 32:32 + AH], nmb))
                dve.tensor_tensor(nmp[:, :, 64:64 + AH], nmr, nmb, ALU.subtract).then_inc(a_nm, 1)
                for half in range(2):
                    dve.wait_ge(a_sm, 2 * n + half + 1)
                    dve.tensor_copy(qst[64 + MAX_ROW:64 + MAX_ROW + 3, 4 * half:4 * half + 4, 1, :],
                                    bank[64 + MAX_ROW:64 + MAX_ROW + 3, 4 * half:4 * half + 4, :]).then_inc(a_mo, 1)
                for j in range(HG):
                    if follow and j < 2:
                        rope(a, b + 1, j)
                    dve.wait_ge(a_pv, n * UNITS + (j + 1) * TILES)
                    dve.tensor_copy(oU[:, j, :], bank[:, 6 + j % 2, :]).then_inc(a_oc, 1)
                for qt in range(TILES):
                    dve.wait_ge(a_ob, n * TILES + qt + 1)
                    o4 = bank[:, qt, :].rearrange("p (j g e) -> p j g e", j=HG, g=4)
                    r3 = rinv[:, qt * AH:(qt + 1) * AH].rearrange("p (j g) -> p j g", j=HG)
                    dve.reciprocal(r3, o4[:, :, :, AD]).then_inc(a_rc, 1)
                    dve.wait_ge(a_rc, n * TILES + qt + 1)
                    if qt >= 2:
                        dve.wait_ge(a_ot, n * TILES + qt - 1)
                    dve.tensor_tensor(on[:, qt % 2, :].rearrange("p (j g d) -> p j g d", g=4, d=AD), o4[:, :, :, 0:AD],
                                      r3.unsqueeze(3).broadcast_to([P, HG, 4, AD]), ALU.mult).then_inc(a_on, 1)
                dve.wait_ge(a_wo, n + 1)
                dve.scalar_tensor_tensor(out=xT[:, b, :], in0=bank[:, 5, :], scalar=bias[:, 9 + 6 * a:10 + 6 * a],
                                         in1=xT[:, b, :], op0=ALU.add, op1=ALU.add).then_inc(step_done, 1)

            dve.wait_ge(ld_c, LOADED)
            dve.wait_ge(x_in, BATCH)
            dve.tensor_copy(maskw[:, :, :].rearrange("p a t -> p (a t)"), mask_f[:, 0:256]).then_inc(masks_set, 1)
            dve.tensor_copy(maskr[:, :], mask_f[:, 256:768]).then_inc(masks_set, 1)
            dve.wait_ge(init, 3)
            dve.wait_ge(masks_set, 2)
            dve.memset(tick[:, :], 0.0).then_inc(step_done, 1)
            attention(0)
            norm_all_vector(dve, SEED)
            ss, nrm = small[:, 0, :], small[:, 1, :]
            mx, den, rden = small[:, 2, 0:LH], small[:, 3, 0:LH], small[:, 4, 0:LH]

            def norm(T):
                ch = Chain(dve, l_chr, T * (NEWTON + 1))
                dve.wait_ge(l_sq, T + 1)
                ch.link(dve.tensor_reduce(ss, sq.rearrange("p (h d) -> p h d", d=LD), AX.X, ALU.add))
                inverse_root(ch, nrm, ss)
                dve.tensor_tensor(qn.rearrange("p (h d) -> p h d", d=LD),
                                  bank[:, 0:4, :].rearrange("p a (h d) -> p (a h) d", d=LD),
                                  nrm.unsqueeze(2).broadcast_to([P, 2 * LH, LD]), ALU.mult).then_inc(l_qn, 1)

            def rotate_1(T, i):
                dve.wait_ge(l_qn, T + 1)
                if not (isinstance(T, int) and T == 0):
                    dve.wait_ge(l_yk, T)
                dve.tensor_tensor(rotA.rearrange("p (a h d) -> p a h d", a=2, h=LH), qn.rearrange("p (a h d) -> p a h d", a=2, h=LH),
                                  rotCl[:, i, :].rearrange("p (a d) -> p a d", a=2).unsqueeze(2).broadcast_to([P, 2, LH, LD]),
                                  ALU.mult).then_inc(l_ra, 1)

            def rotate_2(T):
                dve.wait_ge(l_ra, T + 1)
                dve.wait_ge(l_rb, 2 * T + 2)
                dve.tensor_tensor(rotB[:, 0:INNER], rotA[:, 0:INNER], rotB[:, 0:INNER], ALU.add).then_inc(l_yq, 1)

            def softmax(T):
                ch = Chain(dve, l_chs, T * 3)
                dve.wait_ge(l_s, T + 1)
                s3 = bank[:, 4:6, :].rearrange("p a (h j) -> p (a h) j", j=64)
                ch.link(dve.tensor_reduce(mx, s3, AX.X, ALU.max))
                dve.tensor_tensor(sc[:, 0, :].rearrange("p (h j) -> p h j", j=64), s3,
                                  mx.unsqueeze(2).broadcast_to([P, LH, 64]), ALU.subtract).then_inc(l_e, 1)

            def sums(T):
                ch = Chain(dve, l_chs, T * 3 + 1)
                dve.wait_ge(l_p, T + 1)
                ch.link(dve.tensor_reduce(den, sc[:, 1, :].rearrange("p (h j) -> p h j", j=64), AX.X, ALU.add))
                ch.link(dve.reciprocal(rden, den))

            def normalise(T):
                dve.wait_ge(l_pv, T + 1)
                dve.tensor_tensor(sc[:, 2, :].rearrange("p (h d) -> p h d", d=LD),
                                  bank[:, 4:6, :].rearrange("p a (h d) -> p (a h) d", d=LD),
                                  rden.unsqueeze(2).broadcast_to([P, LH, LD]), ALU.mult).then_inc(l_on, 1)

            def rotate(T, i):
                norm(T)
                rotate_1(T, i)

            def shifted(b):
                dve.tensor_copy(xs[64:P, b % 2, WIN + 1:], zT[64:P, b, 0:SEQ - 1]).then_inc(l_xs, 1)

            def tables(k):
                dve.wait_ge(ld_s, k)
                h = LD // 2
                qk2 = qks[:, :, :]
                dve.tensor_tensor(rotCl[:, :, :].rearrange("p c (a d) -> p c a d", a=2), rotC[:, :, :].rearrange("p c (a d) -> p c a d", a=2),
                                  qk2.unsqueeze(1).broadcast_to([P, TILES, 2, LD]), ALU.mult).then_inc(l_tab, 1)
                for lo in range(2):
                    o, s = (slice(0, h), slice(h, LD)) if lo == 0 else (slice(h, LD), slice(0, h))
                    last = dve.tensor_tensor(rotSl[:, :, :].rearrange("p c (a d) -> p c a d", a=2)[:, :, :, o],
                                             rotS[:, :, :].rearrange("p c (a d) -> p c a d", a=2)[:, :, :, o],
                                             qk2[:, :, s].unsqueeze(1).broadcast_to([P, TILES, 2, h]), ALU.mult)
                    last.then_inc(l_tab, 1)

            def tiles(l, b, tail, follow):
                it = l * BATCH + b
                for i in range(TILES):
                    T = it * TILES + i
                    if tail and i == 0:
                        residual(it - 1, (b - 1) % BATCH)
                    if tail and i == 2:
                        hidden(it - 1, 0)
                        hidden(it - 1, 1)
                    if tail and i == 3:
                        hidden(it - 1, 2)
                    softmax(T)
                    if tail and i == 1:
                        scale_norm(it - 1)
                    sums(T)
                    if i + 1 < TILES or follow:
                        rotate_2(T + 1)
                    normalise(T)
                    if tail and i == 0:
                        centre(it - 1)
                    if tail and i == 3:
                        ffn_end(it - 1, (b - 1) % BATCH)
                    if follow and i == 1:
                        if tail:
                            dve.wait_ge(l_v, 4 * TILES * it)
                            settle(dve)
                        shifted((b + 1) % BATCH)
                    if follow and i == 2 and b == BATCH - 1:
                        tables(l * 32 + 64)
                        dve.wait_ge(l_tab, l * 3 + 6)
                    if i + 2 < TILES or follow:
                        rotate(T + 2, (i + 2) % TILES)

            def residual(it, b):
                dve.wait_ge(l_wo, it + 1)
                dve.tensor_tensor(zT[:, b, :], bank[:, 0, :], zT[:, b, :], ALU.add).then_inc(l_res, 1)
                dve.wait_ge(l_res, it + 1)
                settle(dve)
                dve.memset(xf[64:P, 0:1], 0.0).then_inc(l_xf, 1)
                dve.tensor_copy(xf[64:P, 1:], zT[64:P, b, 0:SEQ - 1]).then_inc(l_xf, 1)

            def centre(it):
                dve.wait_ge(l_xf, 3 * it + 3)
                ln_centre(dve, LAYER0 + it, xf, 7)

            def scale_norm(it):
                ln_scale(dve, LAYER0 + it, sqn[:, :])
                dve.wait_ge(ln_out, LAYER0 + it + 1)
                dve.tensor_scalar(xn[:, :], sqn[:, :], lb[:, 0:1], lb[:, 1:2], ALU.mult, ALU.add).then_inc(l_fn, 1)

            def hidden(it, j):
                n = FCH[j][1]
                dve.wait_ge(f_h, 6 * it + 2 * j + 2)
                dve.wait_ge(f_g, 3 * it + j + 1)
                dve.scalar_tensor_tensor(out=hT[0:n, j, :], in0=bank[0:n, 2 * (j % 2) + 1, :], scalar=lb[0:n, 3 + j:4 + j],
                                         in1=gates[0:n, j, :], op0=ALU.add, op1=ALU.mult).then_inc(f_hd, 1)

            def ffn_end(it, b):
                dve.wait_ge(f_y, it + 1)
                dve.scalar_tensor_tensor(out=zT[:, b, :], in0=bank[:, 7, :], scalar=lb[:, 2:3],
                                         in1=zT[:, b, :], op0=ALU.add, op1=ALU.add).then_inc(step_done, 1)

            dve.wait_ge(step_done, LAYER0 + 1)
            tables(32)
            dve.wait_ge(l_tab, 3)
            shifted(0)
            rotate(0, 0)
            rotate_2(0)
            rotate(1, 1)
            tiles(0, 0, False, True)
            dve.wait_ge(ld_f, LDF)
            with dve.Fori(0, DEPTH - 1) as l:
                for b in range(1, BATCH):
                    tiles(l, b, True, True)
                tiles(l + 1, 0, True, True)
            for b in range(1, BATCH):
                tiles(DEPTH - 1, b, True, b + 1 < BATCH)
            last = DEPTH * BATCH - 1
            residual(last, BATCH - 1)
            centre(last)
            scale_norm(last)
            for j in range(3):
                hidden(last, j)
            ffn_end(last, BATCH - 1)
            with dve.Fori(0, BATCH) as b:
                dve.wait_ge(step_done, ATT1 + 1)
                dve.tensor_tensor(xT[:, b, :], xT[:, b, :], zT[:, b, :], ALU.add).then_inc(x_sum, 1)
            dve.wait_ge(x_sum, BATCH)
            attention(1)
            norm_all_vector(dve, MOE0)

            def g3(j):
                return rt[:, j, :].rearrange("p (i e) -> p i e", e=NE)

            def bc(v):
                return v.unsqueeze(2).broadcast_to([P, NT, NE])

            def per_e(j):
                return moe_c[:, j, :].unsqueeze(1).broadcast_to([P, NT, NE])

            mxl, mxv, sume, prob, s1, r1, keep, wgt = (rs[:, j, 0:NT] for j in range(8))
            ch = Chain(dve, m_ch, 0)
            dve.wait_ge(m_lg, 1)
            lg = bank[:, 2, 0:256].rearrange("p (i e) -> p i e", e=NE)
            ch.link(dve.tensor_reduce(mxl, lg, AX.X, ALU.max))
            dve.tensor_tensor(g3(0), lg, bc(mxl), ALU.subtract).then_inc(m_sh, 1)
            dve.wait_ge(m_sh, 1)
            ch.link(dve.scalar_tensor_tensor(out=g3(2), in0=g3(0), scalar=0.0, in1=per_e(0), op0=ALU.is_equal, op1=ALU.mult))
            ch.link(dve.tensor_reduce(mxv, g3(2), AX.X, ALU.max))
            dve.tensor_tensor(g3(3), g3(2), bc(mxv), ALU.is_equal).then_inc(m_oh, 1)
            dve.wait_ge(m_ex, 1)
            ch.link(dve.tensor_reduce(sume, g3(1), AX.X, ALU.add))
            ch.link(dve.reciprocal(prob, sume))
            ch.link(dve.memset(rt[:, 4, 0:NE], 0.0))
            dve.wait_ge(m_cum, 1)
            for i in range(1, NT):
                ch.link(dve.tensor_tensor(rt[:, 4, i * NE:(i + 1) * NE], rt[:, 4, (i - 1) * NE:i * NE],
                                          bank[:, 0, (i - 1) * NE:i * NE], ALU.add))
            ch.link(dve.tensor_tensor(rt[:, 5, :], rt[:, 4, :], bank[:, 7, 0:256], ALU.add))
            ch.link(dve.tensor_tensor(rt[:, 6, :], rt[:, 5, :], rt[:, 3, :], ALU.mult))
            ch.link(dve.tensor_reduce(r1, g3(6), AX.X, ALU.add))
            ch.link(dve.tensor_tensor(g3(7), g3(5), per_e(1), ALU.add))
            ch.link(dve.tensor_tensor(rt[:, 2, :], rt[:, 7, :], rt[:, 3, :], ALU.mult))
            ch.link(dve.tensor_reduce(s1, g3(2), AX.X, ALU.add))
            ch.link(dve.tensor_scalar(keep, r1, float(CAP), None, ALU.is_le))
            ch.link(dve.tensor_tensor(wgt, keep, prob, ALU.mult))
            ch.link(dve.tensor_tensor(r1, s1, moe_c[:, 2, :], ALU.subtract))
            ch.link(dve.tensor_tensor(r1, r1, keep, ALU.mult))
            ch.link(dve.tensor_tensor(r1, r1, moe_c[:, 2, :], ALU.add))
            dve.tensor_copy(idx[:, 0, :], r1).then_inc(m_idx, 1)
            ch.link(dve.tensor_tensor(s1, s1, keep, ALU.mult))
            dve.tensor_copy(idx[:, 1, :], s1).then_inc(m_idx, 1)
            for e in range(NE):
                dve.wait_ge(m_d, e + 1)
                if e >= 2:
                    dve.wait_ge(m_h, e - 1)
                dve.tensor_copy(dT[:, e % 2, :], bank[:, e % 2, 0:CAP]).then_inc(m_dc, 1)
                if e >= 1:
                    out_rows(dve, e - 1)
            out_rows(dve, NE - 1)
            for q in range(4):
                dve.wait_ge(m_xo, q + 1)
                dve.wait_ge(m_g, 16 * NT)
                for i in range(4 * q, 4 * q + 4):
                    last = dve.scalar_tensor_tensor(out=fin[:, i, :], in0=gat[:, i, :], scalar=wgt[:, i:i + 1],
                                                    in1=bank[:, (6, 7, 0, 1)[q], (i % 4) * P:(i % 4 + 1) * P],
                                                    op0=ALU.mult, op1=ALU.add)
                last.then_inc(m_fin, 1)


def constants():
    f = np.float32
    c = {"c_ident": np.eye(P, dtype=f), "c_mean": np.full((P, P), 1.0 / P, f)}
    c["c_upper"] = np.triu(np.ones((P, P), f))
    pos = np.arange(SEQ, dtype=f)
    ids = np.arange(P // 2, dtype=f)
    theta0 = (f(10000.0) ** (f(-2.0) * ids) / f(P // 2)).astype(f)
    ang0 = (pos[:, None] * theta0[None, :]).astype(f)
    theta1 = (f(10000.0) ** (f(-2.0) * np.arange(AD // 2, dtype=f) / f(AD))).astype(f)
    ang1 = (pos[:, None] * theta1[None, :]).astype(f)
    j = np.arange(P)
    a0, a1 = ang0[:, j // 2].T.astype(np.float64), ang1[:, (j % AD) // 2].T.astype(np.float64)
    s0 = np.where(j % 2 == 0, -1.0, 1.0)[:, None]
    s1 = np.where(j % AD < AD // 2, -1.0, 1.0)[:, None]
    c["c_ropeC"] = np.stack([np.cos(a0), np.cos(a1)], 1).astype(f)
    c["c_ropeS"] = np.stack([np.sin(a0) * s0, np.sin(a1) * s1], 1).astype(f)
    one = np.uint16(0x3F80)
    selm = np.zeros((P, AH, 32), np.uint16)
    for h in range(AH):
        for part in range(3):
            selm[32 * part + h, h, part] = one
    maxrows = np.zeros((2, AD, AH // 2 * SEQ), np.uint16)
    maxrows[1, 0:3] = one
    c["c_maxrows"] = maxrows.view(f)
    c["c_selm"] = selm.reshape(P, 512).view(f)
    half = np.arange(0, LD, 2, dtype=f)
    inv_freq = (f(1.0) / f(10000.0) ** (half / f(LD))).astype(f)
    fr = (pos[:, None] * inv_freq[None, :]).astype(f).astype(np.float64)
    base = ((half + f(0.4 * LD)) / f(1.4 * LD)).astype(f)
    power = ((pos - SEQ // 2) / f(WIN // 2)).astype(f)
    scale = (base[None, :].astype(np.float64) ** power[:, None].astype(np.float64)).astype(f).astype(np.float64)
    tabs = []
    for t, sign in ((np.cos(fr), (1, 1)), (np.sin(fr), (-1, 1))):
        full = []
        for s in (scale, 1.0 / scale):
            full.append(np.concatenate([sign[0] * t * s, sign[1] * t * s], 1))
        tabs.append(np.concatenate(full, 1).reshape(TILES, P, 2 * LD).transpose(1, 0, 2).astype(f))
    c["c_rotC"], c["c_rotS"] = tabs
    w = np.zeros((P, 2, P), f)
    w[np.arange(P) % WIN, :, np.arange(P)] = 1.0
    w[WIN, 0, 0:WIN] = 1.0
    ii, jj = np.arange(WIN)[:, None], np.arange(2 * WIN)[None, :]
    m = np.zeros((P, 2 * WIN), f)
    m[0:WIN] = np.where((jj < ii) | (jj > ii + WIN), f(NEG), f(0.0))
    m[WIN, 0:WIN] = NEG
    c["c_maskw"] = w.reshape(P, 2 * P)
    c["c_maskr"] = np.tile(m, (1, PAIRS)).astype(f)
    e = np.arange(NE, dtype=f)
    moe = np.zeros((P, 3, NE), f)
    moe[:, 0, :] = NE - e
    moe[:, 1, :] = e * CAP - 1
    moe[:, 2, :] = SLOTS + np.arange(NT)[None, :] * P + np.arange(P)[:, None]
    c["c_moe"] = moe
    return c


def kernel(**inputs):
    import concourse.bacc as _bacc
    from concourse.bass_utils import run_bass_kernel_spmd as _run

    swap0 = np.arange(P) ^ 1
    swap1 = (np.arange(P) // AD) * AD + (np.arange(P) % AD + AD // 2) % AD
    a = {n: np.ascontiguousarray(v) for n, v in inputs.items()}
    a.update(constants())
    a["wqr_swapped"] = np.ascontiguousarray(a["L0_attn_Wq_r_w"][:, swap0])
    a["wkr_swapped"] = np.ascontiguousarray(a["L0_attn_Wk_r_w"][:, swap0])
    a["bqr_swapped"] = np.ascontiguousarray(a["L0_attn_Wq_r_b"][swap0])
    a["bkr_swapped"] = np.ascontiguousarray(a["L0_attn_Wk_r_b"][swap0])
    for n in "qkvo":
        a[f"w{n}_t"] = np.ascontiguousarray(a.pop(f"L1_attn_w{n}").T)
    for n in "qk":
        a[f"w{n}_swapped"] = np.ascontiguousarray(a[f"w{n}_t"][:, swap1])
        a[f"b{n}_swapped"] = np.ascontiguousarray(a[f"L1_attn_b{n}"][swap1])
    a["gate_t"] = np.ascontiguousarray(a.pop("L1_ffn_gate_w").T)
    columns = np.zeros((P, len(BIASES)), np.float32)
    for j, n in enumerate(BIASES):
        columns[:len(a[n]), j] = a[n]
    low = np.concatenate([a[n] for n in PACKED_LOW], 1)
    high = np.concatenate([a[m] for n in PACKED for m in n.split("+")], 1)
    for n in set(BIASES + PACKED_LOW + "+".join(PACKED).split("+")):
        del a[n]
    a["bias_columns"], a["packed_low"], a["packed"] = columns, low, high
    nc = _bacc.Bacc("TRN2", target_bir_lowering=False, num_devices=1)
    arrays, aps = {}, {}
    for name, v in a.items():
        arrays[f"in_{name}"] = v
        aps[name] = nc.dram_tensor(f"in_{name}", v.shape, mybir.dt.from_np(v.dtype), kind="ExternalInput").ap()
    out = nc.dram_tensor("out_0", (BATCH, SEQ, P), F32, kind="ExternalOutput").ap()
    build(nc, aps, out)
    r = _run(nc, [arrays], core_ids=[0])
    return r.results[0]["out_0"]
```
